# Optimizing a Trainium2 kernel written in Bass

```python
import numpy as np
import jax
import jax.numpy as jnp

def _softmax(x, axis=-1):
    return jax.nn.softmax(x, axis=axis)

def _gelu(x):
    return jax.nn.gelu(x, approximate=True)

def _silu(x):
    return jax.nn.silu(x)

def _sigmoid(x):
    return jax.nn.sigmoid(x)

def _layernorm(x, axis=-1, eps=1e-05):
    m = jnp.mean(x, axis=axis, keepdims=True)
    v = jnp.var(x, axis=axis, keepdims=True)
    return (x - m) / jnp.sqrt(v + eps)

def _scatter_add(tgt, idx, src, axis=0):
    return tgt.at[idx].add(src)

def _segment_sum(src, seg, n):
    return jax.ops.segment_sum(src, seg, n)
kernel_name = 'mk_adaln_d1_jaxref_r8_64adff'

def setup_inputs(seed: int=0):
    np.random.seed(seed)
    _w = jnp.asarray

    def _L0_attn_setup():
        import jax, jax.numpy as jnp
        import numpy as np
        BATCH, SEQ, D_MODEL, D_STATE = (4, 512, 256, 128)
        key = jax.random.key(seed)
        kx, kb, kc = jax.random.split(key, 3)
        x = jax.random.normal(kx, (BATCH, SEQ, D_MODEL), dtype=jnp.float32)
        B = jax.random.normal(kb, (D_STATE, D_MODEL), dtype=jnp.float32) * 0.01
        C = jax.random.normal(kc, (D_MODEL, D_STATE), dtype=jnp.float32) * 0.01
        D = jnp.zeros((D_MODEL,), dtype=jnp.float32)
        return {'x': x, 'B': B, 'C': C, 'D': D}
    _L0_attn_in = _L0_attn_setup()

    def _L0_ffn_setup():
        import jax, jax.numpy as jnp
        import numpy as np
        B, S, H, I, E = (2, 64, 256, 512, 8)
        JITTER_EPS = 0.01
        NEG_INF = float('-inf')

        def _route(logits):
            max1 = jnp.max(logits, axis=-1, keepdims=True)
            ind1 = jnp.argmax(logits, axis=-1, keepdims=True)
            factor1 = jnp.maximum(jnp.abs(logits), max1)
            mask1 = (max1 - logits) / factor1 > 2.0 * JITTER_EPS
            gates1 = jax.nn.softmax(jnp.where(mask1, NEG_INF, logits), axis=-1)
            mult1 = jnp.take_along_axis(gates1, ind1, axis=-1)
            sel1_onehot = jax.nn.one_hot(ind1[..., 0], E, dtype=jnp.bool_)
            masked_scores = jnp.where(sel1_onehot, NEG_INF, logits)
            max2 = jnp.max(masked_scores, axis=-1, keepdims=True)
            ind2 = jnp.argmax(masked_scores, axis=-1, keepdims=True)
            factor2 = jnp.maximum(jnp.abs(logits), max2)
            mask2 = (max2 - masked_scores) / factor2 > 2.0 * JITTER_EPS
            gates2 = jax.nn.softmax(jnp.where(mask2, NEG_INF, masked_scores), axis=-1)
            mult2 = jnp.take_along_axis(gates2, ind2, axis=-1)
            return (jnp.concatenate([mult1, mult2], axis=-1), jnp.concatenate([ind1, ind2], axis=-1))
        key = jax.random.key(seed)
        ks = jax.random.split(key, 5)
        std = 0.02
        return {'hidden_states': jax.random.normal(ks[0], (B, S, H), jnp.float32), 'gate_w': jax.random.normal(ks[1], (E, H), jnp.float32) * std, 'w1': jax.random.normal(ks[2], (E, I, H), jnp.float32) * std, 'w2': jax.random.normal(ks[3], (E, H, I), jnp.float32) * std, 'w3': jax.random.normal(ks[4], (E, I, H), jnp.float32) * std}
    _L0_ffn_in = _L0_ffn_setup()
    _L0_c = _w((lambda *s: np.random.randn(*s).astype(np.float32) * 0.05)(4, 256))
    _L0_wmod = _w((lambda *s: np.random.randn(*s).astype(np.float32) * 0.05)(256, 6 * 256) * 256 ** (-0.5))
    _d = {'L0_attn_x': _L0_attn_in['x'], 'L0_attn_B': _L0_attn_in['B'], 'L0_attn_C': _L0_attn_in['C'], 'L0_attn_D': _L0_attn_in['D'], 'L0_ffn_gate_w': _L0_ffn_in['gate_w'], 'L0_ffn_w1': _L0_ffn_in['w1'], 'L0_ffn_w2': _L0_ffn_in['w2'], 'L0_ffn_w3': _L0_ffn_in['w3'], 'L0_c': _L0_c, 'L0_wmod': _L0_wmod}
    _x0 = _d['L0_attn_x']
    _d['L0_attn_x'] = jax.random.normal(jax.random.fold_in(jax.random.key(seed), 1), (4, 512, 256), dtype=_x0.dtype)
    del _x0
    return _d

def reference(L0_attn_x, L0_attn_B, L0_attn_C, L0_attn_D, L0_ffn_gate_w, L0_ffn_w1, L0_ffn_w2, L0_ffn_w3, L0_c, L0_wmod):

    def _L0_attn_ref(x, B, C, D):
        import jax, jax.numpy as jnp
        import numpy as np
        BATCH, SEQ, D_MODEL, D_STATE = (4, 512, 256, 128)
        state = jnp.tanh(jnp.einsum('bsd,nd->bsn', x, B))
        return jnp.einsum('bsn,dn->bsd', state, C) + D * x

    def _L0_ffn_ref(hidden_states, gate_w, w1, w2, w3):
        import jax, jax.numpy as jnp
        import numpy as np
        B, S, H, I, E = (2, 64, 256, 512, 8)
        JITTER_EPS = 0.01
        NEG_INF = float('-inf')

        def _route(logits):
            max1 = jnp.max(logits, axis=-1, keepdims=True)
            ind1 = jnp.argmax(logits, axis=-1, keepdims=True)
            factor1 = jnp.maximum(jnp.abs(logits), max1)
            mask1 = (max1 - logits) / factor1 > 2.0 * JITTER_EPS
            gates1 = jax.nn.softmax(jnp.where(mask1, NEG_INF, logits), axis=-1)
            mult1 = jnp.take_along_axis(gates1, ind1, axis=-1)
            sel1_onehot = jax.nn.one_hot(ind1[..., 0], E, dtype=jnp.bool_)
            masked_scores = jnp.where(sel1_onehot, NEG_INF, logits)
            max2 = jnp.max(masked_scores, axis=-1, keepdims=True)
            ind2 = jnp.argmax(masked_scores, axis=-1, keepdims=True)
            factor2 = jnp.maximum(jnp.abs(logits), max2)
            mask2 = (max2 - masked_scores) / factor2 > 2.0 * JITTER_EPS
            gates2 = jax.nn.softmax(jnp.where(mask2, NEG_INF, masked_scores), axis=-1)
            mult2 = jnp.take_along_axis(gates2, ind2, axis=-1)
            return (jnp.concatenate([mult1, mult2], axis=-1), jnp.concatenate([ind1, ind2], axis=-1))
        b, s, h = hidden_states.shape
        x = hidden_states.reshape(-1, h)
        logits = x @ gate_w.T
        mult, sel = _route(logits)
        combine = jnp.einsum('tk,tke->te', mult, jax.nn.one_hot(sel, E, dtype=x.dtype))
        h1 = jnp.einsum('th,eih->eti', x, w1)
        h3 = jnp.einsum('th,eih->eti', x, w3)
        act = jax.nn.silu(h1) * h3
        y = jnp.einsum('eti,ehi->eth', act, w2)
        out = jnp.einsum('eth,te->th', y, combine)
        return out.reshape(b, s, h)
    x = L0_attn_x
    mod = (_silu(L0_c) @ L0_wmod).reshape(L0_c.shape[0], 6, 1, -1)
    sa, ca, ga, sb, cb, gb = (mod[:, 0], mod[:, 1], mod[:, 2], mod[:, 3], mod[:, 4], mod[:, 5])
    ga = (2 * (ga >= 0) - 1) * jnp.maximum(jnp.abs(ga), 0.25)
    gb = (2 * (gb >= 0) - 1) * jnp.maximum(jnp.abs(gb), 0.25)
    h = _layernorm(x, axis=-1) * (1 + ca) + sa
    x = x + ga * _L0_attn_ref(h, L0_attn_B, L0_attn_C, L0_attn_D)
    h = _layernorm(x, axis=-1) * (1 + cb) + sb
    x = x + gb * _L0_ffn_ref(h, L0_ffn_gate_w, L0_ffn_w1, L0_ffn_w2, L0_ffn_w3)
    return x

_drawn_inputs = setup_inputs


def setup_inputs(seed=0):
    import zlib

    import numpy as np

    out = dict(_drawn_inputs(seed))
    spreads = {'L0_attn_D': (0.0, 0.33)}
    factors = {'L0_attn_B': 8.0,
     'L0_attn_C': 8.0,
     'L0_ffn_gate_w': 7.78,
     'L0_ffn_w1': 6.834,
     'L0_ffn_w2': 6.755,
     'L0_ffn_w3': 6.755}
    for name, (base, spread) in spreads.items():
        noise = np.random.default_rng([zlib.crc32(name.encode()), seed]).standard_normal(out[name].shape)
        drawn = base * np.exp(spread * noise) if base else spread * noise
        out[name] = jnp.asarray(drawn.astype(out[name].dtype))
    for name, factor in factors.items():
        out[name] = (out[name] * factor).astype(out[name].dtype)
    return out
```

```python
from contextlib import ExitStack

import concourse.bass as bass
from concourse import mybir

P = 128
BATCH, SEQ, D, NSTATE = 4, 512, 256, 128
E, I, TOPK = 8, 512, 2
TOKENS = BATCH * SEQ
TILES = TOKENS // P
PB = SEQ // P
KD = D // P
KI = I // P
SLOT_TILES = TOKENS * TOPK // P + E - 1
WSTEP = KD * I
assert WSTEP == KI * D
EPS = 1e-5
JITTER2 = 0.02
FAR = -3.0e38

F32 = mybir.dt.float32
BF16 = mybir.dt.bfloat16
I32 = mybir.dt.int32
U32 = mybir.dt.uint32
ALU = mybir.AluOpType
ACT = mybir.ActivationFunctionType
AX_X = mybir.AxisListType.X

C_ID = 0
C_UP = C_ID + P
C_IOTA = C_UP + P
C_TOK = C_IOTA + P
C_TIE = C_TOK + TILES
C_TRASH = C_TIE + E
C_END = C_TRASH + 1


def build(nc, x_in, bT_in, cT_in, dT_in, gw_in, w1_in, w3_in, w2_in, silu_in, wmod_in, const_in, out):
    ctx = ExitStack()
    with ctx:
        def sb(name, cols, dt=F32):
            return ctx.enter_context(nc.sbuf_tensor(name, [P, cols], dt))

        def sem(name):
            return ctx.enter_context(nc.semaphore(name))

        h2_dram = nc.dram_tensor("h2_rows", (TOKENS, D), F32, kind="Internal").ap()
        moe_dram = nc.dram_tensor("moe_sum", (TOKENS + P, D), F32, kind="Internal").ap()
        mod_dram = nc.dram_tensor("mod_rows", (BATCH, 4 * D), F32, kind="Internal").ap()

        w1 = sb("w1", E * WSTEP)
        w3 = sb("w3", E * WSTEP)
        w2 = sb("w2", E * WSTEP)
        x = sb("x", TILES * D)
        wmod = sb("wmod", KD * 6 * D)
        const = sb("const", C_END)
        bT = sb("bT", KD * NSTATE)
        cT = sb("cT", D)
        dT = sb("dT", KD)
        gw = sb("gw", KD * E)
        cond = sb("cond", KD * BATCH)
        cond_silu = sb("cond_silu", KD * BATCH)
        mod_col = sb("mod_col", 6 * BATCH)
        gate_tmp = sb("gate_tmp", 6 * BATCH)
        ga_d = sb("ga_d", KD * BATCH)
        mod_row = sb("mod_row", 4 * D)
        row_tmp = sb("row_tmp", 2 * D)
        mod_all = sb("mod_all", BATCH * 4 * D)
        c_ga = sb("c_ga", BATCH * D)
        diag = sb("diag", BATCH * D)
        zeros = sb("zeros", D)
        stats = sb("stats", PB * 6)
        mean_var = sb("mean_var", PB * 2)
        var_eps = sb("var_eps", PB)
        rstd = sb("rstd", PB)
        stats2 = sb("stats2", PB * 6)
        mean_var2 = sb("mean_var2", PB * 2)
        var_eps2 = sb("var_eps2", PB)
        rstd2 = sb("rstd2", PB)
        minus_half = sb("minus_half", PB)
        xhat = sb("xhat", PB * D)
        hT = sb("hT", KD * SEQ)
        stateT = sb("stateT", SEQ)
        xhat2 = sb("xhat2", PB * D)
        h2m = sb("h2m", PB * D)
        h2 = sb("h2", PB * D)
        h2T = sb("h2T", KD * SEQ)
        TE = TILES * E
        logit = sb("logit", TE)
        logit2 = sb("logit2", TE)
        logit_abs = sb("logit_abs", TE)
        top = sb("top", 2 * TILES)
        tie = sb("tie", 2 * TE)
        tie_max = sb("tie_max", 2 * TILES)
        pick = sb("pick", 2 * TE)
        below = sb("below", 2 * TE)
        scale = sb("scale", 2 * TE)
        keep = sb("keep", 2 * TE)
        expo = sb("expo", 2 * TE)
        expo_sum = sb("expo_sum", 2 * TILES)
        gate = sb("gate", 2 * TILES)
        both = sb("both", TE, BF16)
        upper_b = sb("upper_b", P, BF16)
        ones_b = sb("ones_b", P, BF16)
        cnt_i = sb("cnt_i", E, I32)
        tiles_i = sb("tiles_i", E, I32)
        scan = [sb(f"scan{n}", 2 * E) for n in range(4)]
        first_slot = sb("first_slot", E)
        slot_all = sb("slot_all", TE)
        slot_pick = sb("slot_pick", 2 * TE)
        slot = sb("slot", 2 * TILES)
        slot_i = sb("slot_i", 2 * TILES, I32)
        slot_lo_i = sb("slot_lo_i", 2 * TILES, I32)
        slot_hi_i = sb("slot_hi_i", 2 * TILES, I32)
        slot_lo = sb("slot_lo", 2 * TILES)
        slot_hi = sb("slot_hi", 2 * TILES)
        past = sb("past", SLOT_TILES * E)
        expert_f = sb("expert_f", SLOT_TILES)
        expert_off = sb("expert_off", SLOT_TILES, I32)
        lo_hot = sb("lo_hot", 2 * P)
        hi_val = sb("hi_val", 2 * 2 * SLOT_TILES)
        slot_tab = sb("slot_tab", 2 * SLOT_TILES)
        empty = sb("empty", SLOT_TILES)
        row_from = sb("row_from", SLOT_TILES, U32)
        row_to = sb("row_to", SLOT_TILES, U32)
        slot_tmp = sb("slot_tmp", SLOT_TILES)
        from_now = sb("from_now", 1, U32)
        to_now = sb("to_now", 1, U32)
        rows = sb("rows", D)
        silu = wmod[:, 0:I]
        act_ = wmod[:, I:2 * I]
        actT = wmod[:, 2 * I:2 * I + KI * P]
        rowsT = wmod[:, 2 * I + KI * P:2 * I + KI * P + KD * P]
        y_gated = sb("y_gated", D)

        ident = const[:, C_ID:C_ID + P]
        iota = const[:, C_IOTA:C_IOTA + P]

        bank = [ctx.enter_context(nc.psum_tensor(f"bank{n}", [P, 512], F32)) for n in range(8)]
        xhatT_ps = bank[0:2]
        state_ps = bank[2]
        attn_ps = bank[3:5]
        h2T_ps = bank[5:7]
        logit_ps = bank[7]
        mod_col_ps = bank[7]
        mod_row_ps = bank[5:7]
        rank_ps = bank[2]
        count_ps = bank[7]
        tab_ps = bank[3]
        up1_ps, up3_ps = bank[0], bank[1]
        rowsT_ps = bank[2]
        actT_ps = bank[5]
        y_ps = bank[3]

        const_in_s = sem("const_loaded")
        cond_in = sem("cond_loaded")
        x_first_in = sem("x_batch0_loaded")
        x_rest_in = sem("x_rest_loaded")
        small_in = sem("small_weights_loaded")
        wmod_in_s = sem("wmod_loaded")
        w_in = sem("expert_weights_loaded")
        zeros_set = sem("zeros_set")
        consts_set = sem("pool_constants_set")
        moe_zeroed = sem("moe_sum_zeroed")
        mod_stored = sem("mod_rows_stored")
        mod_spread = sem("mod_rows_spread")
        cond_done = sem("silu_of_cond_done")
        col_ready = sem("mod_col_psum_ready")
        row_ready = sem("mod_row_psum_ready")
        modcol_done = sem("mod_col_done")
        modrow_done = sem("mod_row_done")
        cga_done = sem("c_ga_and_diag_done")
        var_ready = sem("var_eps_ready")
        rstd_ready = sem("rstd_ready")
        var2_ready = sem("var_eps2_ready")
        rstd2_ready = sem("rstd2_ready")
        xhat_ready = sem("xhat_ready")
        xhatT_ready = sem("xhatT_psum_ready")
        hT_ready = sem("hT_ready")
        state_ps_ready = sem("state_psum_ready")
        state_ready = sem("state_ready")
        attn_ready = sem("attn_psum_ready")
        x1_ready = sem("x1_ready")
        h2m_ready = sem("h2_scaled")
        h2_ready = sem("h2_ready")
        h2T_ps_ready = sem("h2T_psum_ready")
        h2T_ready = sem("h2T_ready")
        logits_ready = sem("logits_psum_ready")
        logits_out = sem("logits_copied")
        h2_stored = sem("h2_rows_stored")
        dve_done = sem("vector_step_done")
        below_ready = sem("distances_ready")
        expo_ready = sem("exponentials_ready")
        both_ready = sem("both_choices_ready")
        rank_ready = sem("ranks_ready")
        hot_ready = sem("slot_one_hots_ready")
        hot_used = sem("slot_one_hots_used")
        table_ready = sem("slot_tables_ready")
        idx_ready = sem("row_indices_copied")
        rows_in = sem("rows_gathered")
        rowsT_ps_ready = sem("rowsT_psum_ready")
        rowsT_ready = sem("rowsT_ready")
        up1_ready = sem("up1_psum_ready")
        up3_ready = sem("up3_psum_ready")
        silu_ready = sem("silu_ready")
        act_ready = sem("act_ready")
        actT_ps_ready = sem("actT_psum_ready")
        actT_ready = sem("actT_ready")
        y_ready = sem("y_psum_ready")
        y_gated_ready = sem("y_gated_ready")
        y_added = sem("y_added_to_moe_sum")
        moe_in = [sem(f"moe_sum_loaded{b}") for b in range(BATCH)]
        out_ready = sem("out_ready")
        out_stored = sem("out_stored")

        block = ctx.enter_context(nc.Block())

        moe_sb = w1

        @block.sync
        def _(sp):
            def x_rows(ap, b, n):
                return ap[b * SEQ:(b + n) * SEQ, :].rearrange("(j p) d -> p j d", p=P)

            def tiles(t, b, n):
                return t[:, b * PB * D:(b + n) * PB * D].rearrange("p (j d) -> p j d", d=D)

            sp.dma_start(cond[:, :], silu_in).then_inc(cond_in, 16)
            sp.dma_start(tiles(x, 0, 1), x_rows(x_in, 0, 1)).then_inc(x_first_in, 16)
            sp.dma_start(const[:, :], const_in).then_inc(const_in_s, 16)
            sp.dma_start(wmod[:, :], wmod_in).then_inc(wmod_in_s, 16)
            sp.dma_start(bT[:, :], bT_in).then_inc(small_in, 16)
            sp.dma_start(cT[:, :], cT_in).then_inc(small_in, 16)
            sp.dma_start(dT[:, :], dT_in).then_inc(small_in, 16)
            sp.dma_start(gw[:, :], gw_in).then_inc(small_in, 16)
            sp.dma_start(tiles(x, 1, 3), x_rows(x_in, 1, 3)).then_inc(x_rest_in, 16)
            sp.wait_ge(modrow_done, 1)
            sp.dma_start(mod_dram, mod_row[0:BATCH, :]).then_inc(mod_stored, 16)
            sp.wait_ge(mod_stored, 16)
            sp.dma_start(mod_all[:, :], mod_dram.rearrange("(a b) c -> a (b c)", a=1).to_broadcast((P, BATCH * 4 * D)))\
                .then_inc(mod_spread, 16)
            for w, w_dram in ((w1, w1_in), (w3, w3_in), (w2, w2_in)):
                sp.dma_start(w[:, :], w_dram, max_dma_last_dim=4096).then_inc(w_in, 16)
            sp.wait_ge(zeros_set, 1)
            sp.dma_start(moe_dram.rearrange("(j p) d -> p j d", p=P),
                         zeros[:, :].unsqueeze(1).to_broadcast((P, TILES + 1, D))).then_inc(moe_zeroed, 16)
            with sp.Fori(0, BATCH) as b:
                sp.wait_ge(h2_ready, b + 1)
                sp.dma_start(h2_dram[bass.ds(b * SEQ, SEQ), :].rearrange("(j p) d -> p j d", p=P),
                             h2[:, :].rearrange("p (j d) -> p j d", d=D)).then_inc(h2_stored, 16)
            sp.wait_ge(y_added, 16 * SLOT_TILES)
            for b in range(BATCH):
                sp.dma_start(tiles(moe_sb, b, 1), x_rows(moe_dram, b, 1)).then_inc(moe_in[b], 16)
            for b in range(BATCH):
                sp.wait_ge(out_ready, b + 1)
                sp.dma_start(x_rows(out, b, 1), tiles(x, b, 1)).then_inc(out_stored, 16)
            sp.wait_ge(out_stored, 16 * BATCH)

        @block.gpsimd
        def _(pool):
            pool.memset(zeros[:, :], 0.0).then_inc(zeros_set, 1)
            pool.memset(minus_half[:, :], -0.5).then_inc(consts_set, 1)
            pool.memset(ones_b[:, :], 1.0).then_inc(consts_set, 1)
            for n in range(4):
                pool.memset(scan[n][:, 0:E], 0.0).then_inc(consts_set, 1)
            pool.wait_ge(consts_set, 6)

            def power(n, ready, done, out_, in_):
                pool.wait_ge(ready, n)
                pool.tensor_tensor(out_[:, :], in_[:, :], minus_half[:, :], ALU.pow).then_inc(done, 1)

            def shift_h2(b):
                pool.wait_ge(h2m_ready, b + 1)
                pool.tensor_tensor(h2[:, :].rearrange("p (j d) -> p j d", d=D),
                                   h2m[:, :].rearrange("p (j d) -> p j d", d=D),
                                   mod_all[:, bass.ds(b * (4 * D) + D, D)].unsqueeze(1).to_broadcast((P, PB, D)),
                                   ALU.add).then_inc(h2_ready, 1)

            power(1, var_ready, rstd_ready, rstd, var_eps)
            pool.wait_ge(mod_spread, 16)
            power(2, var_ready, rstd_ready, rstd, var_eps)
            power(1, var2_ready, rstd2_ready, rstd2, var_eps2)
            shift_h2(0)
            with pool.Fori(1, BATCH - 1) as b:
                power(b + 2, var_ready, rstd_ready, rstd, var_eps)
                power(b + 1, var2_ready, rstd2_ready, rstd2, var_eps2)
                pool.wait_ge(h2T_ps_ready, KD * b)
                pool.wait_ge(h2_stored, 16 * b)
                shift_h2(b)
            power(BATCH, var2_ready, rstd2_ready, rstd2, var_eps2)
            pool.wait_ge(h2T_ps_ready, KD * (BATCH - 1))
            pool.wait_ge(h2_stored, 16 * (BATCH - 1))
            shift_h2(BATCH - 1)

            def copy_index(now, table, s, count):
                pool.tensor_copy(now[:, :], table[:, bass.ds(s, 1)]).then_inc(idx_ready, 1)
                if not isinstance(count, int):
                    pool.reg_add(copies, copies, 1)
                    count = copies
                pool.wait_ge(moe_zeroed, 16)
                pool.wait_ge(idx_ready, count)

            def fetch(s, count):
                copy_index(from_now, row_from, s, count)
                pool.indirect_dma_start(rows[:, :], None, h2_dram,
                                        bass.IndirectOffsetOnAxis(ap=from_now[:, :], axis=0)).then_inc(rows_in, 16)

            def add_back(s, count):
                pool.wait_ge(y_gated_ready, s + 1)
                copy_index(to_now, row_to, s, count)
                pool.indirect_dma_start(moe_dram, bass.IndirectOffsetOnAxis(ap=to_now[:, :], axis=0), y_gated[:, :],
                                        None, compute_op=ALU.add).then_inc(y_added, 16)

            pool.wait_ge(table_ready, 1)
            pool.wait_ge(h2_stored, 16 * BATCH)
            pool.wait_ge(moe_zeroed, 16)
            fetch(0, 1)
            pool.wait_ge(rowsT_ps_ready, 1)
            fetch(1, 2)
            pool.wait_ge(rowsT_ps_ready, 2)
            fetch(2, 3)
            add_back(0, 4)
            copies = pool.alloc_register("index_copies")
            pool.reg_mov(copies, 4)
            with pool.Fori(2, SLOT_TILES - 1) as s:
                pool.wait_ge(rowsT_ps_ready, s + 1)
                fetch(s + 1, copies)
                pool.wait_ge(y_added, 16 * (s - 1))
                add_back(s - 1, copies)
            for s in (SLOT_TILES - 2, SLOT_TILES - 1):
                pool.wait_ge(y_added, 16 * s)
                add_back(s, SLOT_TILES + 1 + s)

        @block.scalar
        def _(act):
            act.wait_ge(cond_in, 16)
            act.activation(cond_silu[:, :], cond[:, :], ACT.Silu).then_inc(cond_done, 1)

            def modulate(b):
                for k in range(KD):
                    act.wait_ge(xhatT_ready, KD * b + k + 1)
                    act.activation(hT[:, k * SEQ:(k + 1) * SEQ], xhatT_ps[k][:, :], ACT.Identity,
                                   bias=mod_col[:, bass.ds(b + k * BATCH, 1)],
                                   scale=mod_col[:, bass.ds(b + (KD + k) * BATCH, 1)]).then_inc(hT_ready, 1)

            def state(b):
                act.wait_ge(state_ps_ready, b + 1)
                act.activation(stateT[:, :], state_ps[:, :], ACT.Tanh).then_inc(state_ready, 1)

            def copy_h2T(b):
                for k in range(KD):
                    act.wait_ge(h2T_ps_ready, KD * b + k + 1)
                    act.activation(h2T[:, k * SEQ:(k + 1) * SEQ], h2T_ps[k][:, :], ACT.Copy).then_inc(h2T_ready, 1)

            act.wait_ge(modcol_done, 1)
            modulate(0)
            state(0)
            with act.Fori(0, BATCH - 1) as b:
                act.wait_ge(attn_ready, 2 * (b + 1))
                modulate(b + 1)
                state(b + 1)
                copy_h2T(b)
            copy_h2T(BATCH - 1)

            for c in range(TOPK):
                act.wait_ge(below_ready, c + 1)
                act.activation(expo[:, c * TE:(c + 1) * TE], below[:, c * TE:(c + 1) * TE], ACT.Exp,
                               scale=-1.0).then_inc(expo_ready, 1)

            def copy_rowsT(s):
                act.wait_ge(rowsT_ps_ready, s + 1)
                act.activation(rowsT[:, :], rowsT_ps[:, 0:KD * P], ACT.Copy).then_inc(rowsT_ready, 1)

            copy_rowsT(0)

            def tile(s, more):
                act.wait_ge(up1_ready, s + 1)
                act.activation(silu[:, :], up1_ps[:, :], ACT.Silu).then_inc(silu_ready, 1)
                if more:
                    copy_rowsT(s + 1)
                act.wait_ge(actT_ps_ready, s + 1)
                act.activation(actT[:, :], actT_ps[:, :], ACT.Copy).then_inc(actT_ready, 1)

            with act.Fori(0, SLOT_TILES - 1) as s:
                tile(s, True)
            tile(SLOT_TILES - 1, False)

        @block.tensor
        def _(pe):
            pe.wait_ge(cond_done, 1)
            pe.wait_ge(wmod_in_s, 16)
            for m in range(3 * KD):
                for k in range(KD):
                    last = pe.matmul(mod_col_ps[:, m * BATCH:(m + 1) * BATCH],
                                     wmod[:, k * 6 * D + m * P:k * 6 * D + (m + 1) * P],
                                     cond_silu[:, k * BATCH:(k + 1) * BATCH], start=(k == 0), stop=(k == KD - 1))
            last.then_inc(col_ready, 1)
            for n in range(2):
                for k in range(KD):
                    last = pe.matmul(mod_row_ps[n][0:BATCH, :], cond_silu[:, k * BATCH:(k + 1) * BATCH],
                                     wmod[:, k * 6 * D + (1 + n) * 512:k * 6 * D + (2 + n) * 512],
                                     start=(k == 0), stop=(k == KD - 1))
            last.then_inc(row_ready, 1)

            def transpose_xhat(b):
                pe.wait_ge(xhat_ready, b + 1)
                for k in range(KD):
                    for q in range(PB):
                        last = pe.transpose(xhatT_ps[k][:, q * P:(q + 1) * P],
                                            xhat[:, q * D + k * P:q * D + (k + 1) * P], ident)
                    last.then_inc(xhatT_ready, 1)

            def state_in(b):
                for k in range(KD):
                    pe.wait_ge(hT_ready, KD * b + k + 1)
                    last = pe.matmul(state_ps[:, :], bT[:, k * NSTATE:(k + 1) * NSTATE], hT[:, k * SEQ:(k + 1) * SEQ],
                                     start=(k == 0), stop=(k == KD - 1))
                last.then_inc(state_ps_ready, 1)

            def attn(b):
                pe.wait_ge(state_ready, b + 1)
                for q in range(PB):
                    o = attn_ps[q // 2]
                    c0 = (q % 2) * D
                    pe.matmul(o[:, c0:c0 + D], stateT[:, q * P:(q + 1) * P], c_ga[:, bass.ds(b * D, D)],
                              start=True, stop=False)
                    for k in range(KD):
                        last = pe.matmul(o[:, c0 + k * P:c0 + (k + 1) * P], hT[:, k * SEQ + q * P:k * SEQ + (q + 1) * P],
                                         diag[:, bass.ds(b * D + k * P, P)], start=False, stop=(k == KD - 1))
                    if q % 2:
                        last.then_inc(attn_ready, 1)

            def transpose_h2(b):
                pe.wait_ge(h2_ready, b + 1)
                for k in range(KD):
                    for q in range(PB):
                        last = pe.transpose(h2T_ps[k][:, q * P:(q + 1) * P],
                                            h2[:, q * D + k * P:q * D + (k + 1) * P], ident)
                    last.then_inc(h2T_ps_ready, 1)

            def logits(b):
                pe.wait_ge(h2T_ready, KD * (b + 1))
                for q in range(PB):
                    for k in range(KD):
                        last = pe.matmul(logit_ps[:, q * E:(q + 1) * E],
                                         h2T[:, k * SEQ + q * P:k * SEQ + (q + 1) * P], gw[:, k * E:(k + 1) * E],
                                         start=(k == 0), stop=(k == KD - 1))
                last.then_inc(logits_ready, 1)

            pe.wait_ge(const_in_s, 16)
            pe.wait_ge(small_in, 64)
            transpose_xhat(0)
            state_in(0)
            pe.wait_ge(cga_done, 1)
            attn(0)
            transpose_xhat(1)
            state_in(1)
            transpose_h2(0)
            logits(0)
            with pe.Fori(1, BATCH - 1) as b:
                pe.wait_ge(x1_ready, 2 * b)
                attn(b)
                transpose_xhat(b + 1)
                state_in(b + 1)
                transpose_h2(b)
                pe.wait_ge(logits_out, b)
                logits(b)
            pe.wait_ge(x1_ready, 2 * (BATCH - 1))
            attn(BATCH - 1)
            transpose_h2(BATCH - 1)
            pe.wait_ge(logits_out, BATCH - 1)
            logits(BATCH - 1)

            pe.wait_ge(both_ready, 1)
            pe.matmul(rank_ps[:, 0:TE], upper_b[:, :], both[:, :], start=True, stop=False)
            for d in range(1, TILES):
                last = pe.matmul(rank_ps[:, d * E:TE], ones_b[:, :], both[:, 0:TE - d * E],
                                 start=False, stop=(d == TILES - 1))
            for j in range(TILES):
                last = pe.matmul(count_ps[:, 0:E], ones_b[:, :], both[:, j * E:(j + 1) * E],
                                 start=(j == 0), stop=(j == TILES - 1))
            last.then_inc(rank_ready, 1)
            for n in range(2 * TILES):
                pe.wait_ge(hot_ready, n + 1)
                h = n % 2
                last = pe.matmul(tab_ps[:, 0:2 * SLOT_TILES], lo_hot[:, h * P:(h + 1) * P],
                                 hi_val[:, h * 2 * SLOT_TILES:(h + 1) * 2 * SLOT_TILES],
                                 start=(n == 0), stop=(n == 2 * TILES - 1))
                last.then_inc(hot_used, 1)

            def transpose_rows(s):
                pe.wait_ge(rows_in, 16 * (s + 1))
                for k in range(KD):
                    last = pe.transpose(rowsT_ps[:, k * P:(k + 1) * P], rows[:, k * P:(k + 1) * P], ident)
                last.then_inc(rowsT_ps_ready, 1)

            def up(s, off):
                pe.wait_ge(rowsT_ready, s + 1)
                for w, ps, done in ((w1, up1_ps, up1_ready), (w3, up3_ps, up3_ready)):
                    for k in range(KD):
                        last = pe.matmul(ps[:, :], rowsT[:, k * P:(k + 1) * P], w[:, bass.ds(off + k * I, I)],
                                         start=(k == 0), stop=(k == KD - 1))
                    last.then_inc(done, 1)

            def down(s, off):
                pe.wait_ge(actT_ready, s + 1)
                for k in range(KI):
                    last = pe.matmul(y_ps[:, 0:D], actT[:, k * P:(k + 1) * P], w2[:, bass.ds(off + k * D, D)],
                                     start=(k == 0), stop=(k == KI - 1))
                last.then_inc(y_ready, 1)

            def transpose_act(s):
                pe.wait_ge(act_ready, s + 1)
                for k in range(KI):
                    last = pe.transpose(actT_ps[:, k * P:(k + 1) * P], act_[:, k * P:(k + 1) * P], ident)
                last.then_inc(actT_ps_ready, 1)

            def weight_column(s):
                return pe.value_load(expert_off[0:1, bass.ds(s, 1)], min_val=0, max_val=(E - 1) * WSTEP)

            pe.wait_ge(w_in, 48)
            transpose_rows(0)
            up(0, weight_column(0))
            transpose_rows(1)
            transpose_act(0)
            up(1, weight_column(1))
            transpose_rows(2)
            down(0, weight_column(0))
            transpose_act(1)
            with pe.Fori(2, SLOT_TILES - 1) as s:
                up(s, weight_column(s))
                transpose_rows(s + 1)
                pe.wait_ge(y_gated_ready, s - 1)
                down(s - 1, weight_column(s - 1))
                transpose_act(s)
            last_tile = SLOT_TILES - 1
            up(last_tile, weight_column(last_tile))
            pe.wait_ge(y_gated_ready, last_tile - 1)
            down(last_tile - 1, weight_column(last_tile - 1))
            transpose_act(last_tile)
            pe.wait_ge(y_gated_ready, last_tile)
            down(last_tile, weight_column(last_tile))

        @block.vector
        def _(dve):
            steps = [0]

            def link(ins, base=None):
                steps[0] += 1
                ins.then_inc(dve_done, 1)
                if base is None:
                    dve.wait_ge(dve_done, steps[0])
                else:
                    dve.reg_add(base, base, 1)
                    dve.wait_ge(x_first_in, 16)
                    dve.wait_ge(dve_done, base)

            def norm_stats(base, col0, st, mv, ve, done):
                for q in range(PB):
                    dve_last = dve.bn_stats(st[:, q * 6:(q + 1) * 6], x[:, bass.ds(col0 + q * D, D)])
                link(dve_last, base)
                for q in range(PB):
                    dve_last = dve.bn_aggr(mv[:, q * 2:(q + 1) * 2], st[:, q * 6:(q + 1) * 6])
                link(dve_last, base)
                dve.tensor_scalar(ve[:, :], mv[:, 1:2 * PB:2], EPS, None, ALU.add).then_inc(done, 1)

            def front_stats(b, base=None):
                norm_stats(base, b * (PB * D), stats, mean_var, var_eps, var_ready)

            def front(b, base=None):
                front_stats(b, base)
                dve.wait_ge(rstd_ready, b + 1)
                for q in range(PB):
                    last = dve.tensor_scalar(xhat[:, q * D:(q + 1) * D], x[:, bass.ds(b * (PB * D) + q * D, D)],
                                             mean_var[:, 2 * q:2 * q + 1], rstd[:, q:q + 1],
                                             ALU.subtract, ALU.mult)
                last.then_inc(xhat_ready, 1)

            def back(b, base=None):
                for g in range(2):
                    dve.wait_ge(attn_ready, 2 * b + g + 1)
                    xs = x[:, bass.ds(b * (PB * D) + g * 2 * D, 2 * D)]
                    link_ins = dve.tensor_tensor(xs, attn_ps[g][:, :], xs, ALU.add)
                    link_ins.then_inc(x1_ready, 1)
                if base is None:
                    dve.wait_ge(x1_ready, 2 * b + 2)
                else:
                    dve.reg_add(x1_count, x1_count, 2)
                    dve.wait_ge(x_first_in, 16)
                    dve.wait_ge(x1_ready, x1_count)
                norm_stats(base, b * (PB * D), stats2, mean_var2, var_eps2, var2_ready)
                dve.wait_ge(rstd2_ready, b + 1)
                for q in range(PB):
                    last = dve.tensor_scalar(xhat2[:, q * D:(q + 1) * D], x[:, bass.ds(b * (PB * D) + q * D, D)],
                                             mean_var2[:, 2 * q:2 * q + 1], rstd2[:, q:q + 1],
                                             ALU.subtract, ALU.mult)
                link(last, base)
                dve.tensor_tensor(h2m[:, :].rearrange("p (j d) -> p j d", d=D),
                                  xhat2[:, :].rearrange("p (j d) -> p j d", d=D),
                                  mod_all[:, bass.ds(b * (4 * D) + 2 * D, D)].unsqueeze(1).to_broadcast((P, PB, D)),
                                  ALU.mult).then_inc(h2m_ready, 1)
                dve.wait_ge(logits_ready, b + 1)
                dve.tensor_copy(logit[:, bass.ds(b * (PB * E), PB * E)], logit_ps[:, 0:PB * E])\
                    .then_inc(logits_out, 1)

            def clamp_gate(out_, in_, t_sign, t_abs):
                dve.tensor_scalar(t_sign, in_, 0.0, 2.0, ALU.is_ge, ALU.mult)
                link(dve.tensor_copy(out_, in_))
                link(dve.scalar_tensor_tensor(t_abs, out_, -1.0, out_, ALU.mult, ALU.max))
                link(dve.tensor_scalar(t_abs, t_abs, 0.25, None, ALU.max))
                return dve.scalar_tensor_tensor(out_, t_sign, -1.0, t_abs, ALU.add, ALU.mult)

            dve.wait_ge(x_first_in, 16)
            front(0)
            dve.wait_ge(const_in_s, 16)
            dve.tensor_copy(upper_b[:, :], const[:, C_UP:C_UP + P])

            W = KD * BATCH
            dve.wait_ge(col_ready, 1)
            dve.tensor_scalar(mod_col[:, W:2 * W], mod_col_ps[:, W:2 * W], 1.0, None, ALU.add)
            link(dve.tensor_copy(mod_col[:, 0:W], mod_col_ps[:, 0:W]))
            link(clamp_gate(mod_col[:, 2 * W:3 * W], mod_col_ps[:, 2 * W:3 * W], gate_tmp[:, 0:W], gate_tmp[:, W:2 * W]))
            dve.wait_ge(small_in, 64)
            dve.tensor_tensor(ga_d[:, :].rearrange("p (k b) -> p k b", b=BATCH),
                              mod_col[:, 2 * W:3 * W].rearrange("p (k b) -> p k b", b=BATCH),
                              dT[:, :].unsqueeze(2).to_broadcast((P, KD, BATCH)), ALU.mult).then_inc(modcol_done, 1)
            dve.wait_ge(modcol_done, 1)
            dve.wait_ge(row_ready, 1)
            g0, g1 = mod_row_ps[0], mod_row_ps[1]
            dve.tensor_copy(mod_row[0:BATCH, D:2 * D], g0[0:BATCH, D:2 * D])
            dve.tensor_scalar(mod_row[0:BATCH, 2 * D:3 * D], g1[0:BATCH, 0:D], 1.0, None, ALU.add)
            link(clamp_gate(mod_row[0:BATCH, 0:D], g0[0:BATCH, 0:D], row_tmp[0:BATCH, 0:D], row_tmp[0:BATCH, D:2 * D]))
            clamp_gate(mod_row[0:BATCH, 3 * D:4 * D], g1[0:BATCH, D:2 * D], row_tmp[0:BATCH, 0:D],
                       row_tmp[0:BATCH, D:2 * D]).then_inc(modrow_done, 1)
            for b in range(BATCH):
                for k in range(KD):
                    dve.tensor_scalar(diag[:, b * D + k * P:b * D + (k + 1) * P], ident,
                                      ga_d[:, k * BATCH + b:k * BATCH + b + 1], None, ALU.mult)
            dve.wait_ge(mod_spread, 16)
            dve.tensor_tensor(c_ga[:, :].rearrange("p (b d) -> p b d", d=D),
                              cT[:, :].unsqueeze(1).to_broadcast((P, BATCH, D)),
                              mod_all[:, :].rearrange("p (b m) -> p b m", b=BATCH)[:, :, 0:D],
                              ALU.mult).then_inc(cga_done, 1)
            dve.wait_ge(x_rest_in, 16)
            dve.wait_ge(xhatT_ready, KD)
            front(1)
            back(0)
            before = steps[0]
            per = 5
            base = dve.alloc_register("vector_steps")
            x1_count = dve.alloc_register("x1_parts")
            dve.reg_mov(base, before)
            dve.reg_mov(x1_count, 2)
            with dve.Fori(1, BATCH - 1) as b:
                dve.wait_ge(x_rest_in, 16)
                dve.wait_ge(xhatT_ready, KD * b + KD)
                front(b + 1, base)
                back(b, base)
            assert steps[0] - before == per, steps[0] - before
            steps[0] = before + per * (BATCH - 2)
            back(BATCH - 1)
            dve.wait_ge(logits_out, BATCH)

            def te(t, c=0):
                return t[:, c * TE:(c + 1) * TE].rearrange("p (j e) -> p j e", e=E)

            def tj(t, c=0):
                return t[:, c * TILES:(c + 1) * TILES]

            def over_e(ap):
                return ap.unsqueeze(2).to_broadcast((P, TILES, E))

            tie_w = const[:, C_TIE:C_TIE + E].unsqueeze(1).to_broadcast((P, TILES, E))
            link(dve.scalar_tensor_tensor(logit_abs[:, :], logit[:, :], -1.0, logit[:, :], ALU.mult, ALU.max))
            for c in range(TOPK):
                score = logit if c == 0 else logit2
                link(dve.tensor_reduce(tj(top, c), te(score), AX_X, ALU.max))
                dve.tensor_tensor(te(below, c), over_e(tj(top, c)), te(score), ALU.subtract).then_inc(below_ready, 1)
                dve.tensor_tensor(te(scale, c), te(logit_abs), over_e(tj(top, c)), ALU.max)
                link(dve.tensor_tensor(te(pick, c), te(score), over_e(tj(top, c)), ALU.is_equal))
                link(dve.tensor_tensor(te(tie, c), te(pick, c), tie_w, ALU.mult))
                link(dve.tensor_reduce(tj(tie_max, c), te(tie, c), AX_X, ALU.max))
                link(dve.tensor_tensor(te(pick, c), te(tie, c), over_e(tj(tie_max, c)), ALU.is_equal))
                dve.scalar_tensor_tensor(keep[:, c * TE:(c + 1) * TE], scale[:, c * TE:(c + 1) * TE], JITTER2,
                                         below[:, c * TE:(c + 1) * TE], ALU.mult, ALU.is_ge)
                if c == 0:
                    link(dve.scalar_tensor_tensor(logit2[:, :], pick[:, 0:TE], FAR, logit[:, :], ALU.mult, ALU.add))
            dve.tensor_tensor(both[:, :], pick[:, 0:TE], pick[:, TE:2 * TE], ALU.add).then_inc(both_ready, 1)
            dve.wait_ge(both_ready, 1)
            dve.wait_ge(expo_ready, TOPK)
            link(dve.tensor_tensor(keep[:, :], keep[:, :], expo[:, :], ALU.mult))
            link(dve.tensor_reduce(expo_sum[:, :], keep[:, :].rearrange("p (j e) -> p j e", e=E), AX_X, ALU.add))
            link(dve.reciprocal(gate[:, :], expo_sum[:, :]))
            dve.wait_ge(rank_ready, 1)
            dve.wait_ge(consts_set, 6)
            link(dve.tensor_scalar(cnt_i[:, :], count_ps[:, 0:E], float(P - 1), None, ALU.add))
            link(dve.tensor_scalar(tiles_i[:, :], cnt_i[:, :], 7, None, ALU.arith_shift_right))
            link(dve.tensor_copy(scan[0][:, E:2 * E], tiles_i[:, :]))
            for n, d in enumerate((1, 2, 4)):
                link(dve.tensor_tensor(scan[n + 1][:, E:2 * E], scan[n][:, E:2 * E], scan[n][:, E - d:2 * E - d],
                                       ALU.add))
            end_tile = scan[3][:, E:2 * E]
            link(dve.tensor_tensor(first_slot[:, :], end_tile, scan[0][:, E:2 * E], ALU.subtract))
            link(dve.scalar_tensor_tensor(te(slot_all), first_slot[:, :].unsqueeze(1).to_broadcast((P, TILES, E)),
                                          float(P), te(rank_ps), ALU.mult, ALU.add))
            for c in range(TOPK):
                last = dve.tensor_tensor(te(slot_pick, c), te(pick, c), te(slot_all), ALU.mult)
            link(last)
            link(dve.tensor_reduce(slot[:, :], slot_pick[:, :].rearrange("p (j e) -> p j e", e=E), AX_X, ALU.add))
            link(dve.tensor_copy(slot_i[:, :], slot[:, :]))
            dve.tensor_scalar(slot_lo_i[:, :], slot_i[:, :], P - 1, None, ALU.bitwise_and)
            link(dve.tensor_scalar(slot_hi_i[:, :], slot_i[:, :], 7, None, ALU.arith_shift_right))
            dve.tensor_copy(slot_lo[:, :], slot_lo_i[:, :])
            link(dve.tensor_copy(slot_hi[:, :], slot_hi_i[:, :]))
            link(dve.tensor_tensor(past[0:1, :].rearrange("p (s e) -> p s e", e=E),
                                   iota[0:1, 0:SLOT_TILES].unsqueeze(2).to_broadcast((1, SLOT_TILES, E)),
                                   end_tile[0:1, :].unsqueeze(1).to_broadcast((1, SLOT_TILES, E)), ALU.is_ge))
            link(dve.tensor_reduce(expert_f[0:1, :], past[0:1, :].rearrange("p (s e) -> p s e", e=E), AX_X, ALU.add))
            dve.tensor_scalar(expert_off[0:1, :], expert_f[0:1, :], float(E - 1), float(WSTEP), ALU.min, ALU.mult)
            for n in range(2 * TILES):
                h = n % 2
                j = n % TILES
                if n >= 2:
                    dve.wait_ge(hot_used, n - 1)
                v0 = h * 2 * SLOT_TILES
                dve.tensor_scalar(lo_hot[:, h * P:(h + 1) * P], iota, slot_lo[:, n:n + 1], None, ALU.is_equal)
                dve.tensor_scalar(hi_val[:, v0:v0 + SLOT_TILES], iota[:, 0:SLOT_TILES], slot_hi[:, n:n + 1],
                                  const[:, C_TOK + j:C_TOK + j + 1], ALU.is_equal, ALU.mult)
                dve.tensor_scalar(hi_val[:, v0 + SLOT_TILES:v0 + 2 * SLOT_TILES], iota[:, 0:SLOT_TILES],
                                  slot_hi[:, n:n + 1], gate[:, n:n + 1], ALU.is_equal, ALU.mult)\
                    .then_inc(hot_ready, 1)
            dve.wait_ge(hot_used, 2 * TILES)
            link(dve.tensor_copy(slot_tab[:, :], tab_ps[:, 0:2 * SLOT_TILES]))
            token1 = slot_tab[:, 0:SLOT_TILES]
            dve.tensor_scalar(row_from[:, :], token1, -1.0, 0.0, ALU.add, ALU.max)
            link(dve.tensor_scalar(empty[:, :], token1, 0.0, const[:, C_TRASH:C_TRASH + 1], ALU.is_equal, ALU.mult))
            dve.scalar_tensor_tensor(row_to[:, :], token1, -1.0, empty[:, :], ALU.add, ALU.add)\
                .then_inc(table_ready, 1)

            def gate_up(s):
                dve.wait_ge(silu_ready, s + 1)
                dve.wait_ge(up3_ready, s + 1)
                dve.tensor_tensor(act_[:, :], silu[:, :], up3_ps[:, :], ALU.mult).then_inc(act_ready, 1)

            def gate_y(s, wait_added=True):
                dve.wait_ge(y_ready, s + 1)
                if wait_added:
                    dve.wait_ge(y_added, 16 * s)
                dve.tensor_scalar(y_gated[:, :], y_ps[:, 0:D], slot_tab[:, bass.ds(s + SLOT_TILES, 1)], None,
                                  ALU.mult).then_inc(y_gated_ready, 1)

            gate_up(0)
            gate_up(1)
            gate_y(0, False)
            with dve.Fori(2, SLOT_TILES) as s:
                gate_up(s)
                gate_y(s - 1)
            gate_y(SLOT_TILES - 1)

            for b in range(BATCH):
                dve.wait_ge(moe_in[b], 16)
                m = moe_sb[:, b * PB * D:(b + 1) * PB * D]
                m3 = m.rearrange("p (j d) -> p j d", d=D)
                gb = mod_all[:, b * 4 * D + 3 * D:(b + 1) * 4 * D].unsqueeze(1).to_broadcast((P, PB, D))
                link(dve.tensor_tensor(m3, m3, gb, ALU.mult))
                xs = x[:, b * PB * D:(b + 1) * PB * D]
                dve.tensor_tensor(xs, xs, m, ALU.add).then_inc(out_ready, 1)


def kernel(**inputs):
    import numpy as np
    import concourse.bacc as bacc
    from concourse.bass_utils import run_bass_kernel_spmd

    def rows_by_chunk(a):
        c = a.shape[0] // P
        return np.ascontiguousarray(a.reshape(c, P, -1).transpose(1, 0, 2).reshape(P, -1))

    def experts(a):
        t = a.transpose(0, 2, 1)
        e, n, m = t.shape
        return np.ascontiguousarray(t.reshape(e, n // P, P, m).transpose(2, 0, 1, 3).reshape(P, -1))

    arr = {k: np.asarray(v) for k, v in inputs.items()}
    const = np.zeros((P, C_END), np.float32)
    const[:, C_ID:C_ID + P] = np.eye(P)
    const[:, C_UP:C_UP + P] = np.triu(np.ones((P, P)), 1)
    const[:, C_IOTA:C_IOTA + P] = np.arange(P)
    const[:, C_TOK:C_TOK + TILES] = 1 + np.arange(P)[:, None] + P * np.arange(TILES)
    const[:, C_TIE:C_TIE + E] = E - np.arange(E)
    const[:, C_TRASH] = TOKENS + 1 + np.arange(P)
    feeds = {
        "x_in": np.ascontiguousarray(arr["L0_attn_x"].reshape(TOKENS, D)),
        "bT_in": rows_by_chunk(arr["L0_attn_B"].T),
        "cT_in": np.ascontiguousarray(arr["L0_attn_C"].T),
        "dT_in": rows_by_chunk(arr["L0_attn_D"].reshape(D, 1)),
        "gw_in": rows_by_chunk(arr["L0_ffn_gate_w"].T),
        "w1_in": experts(arr["L0_ffn_w1"]),
        "w3_in": experts(arr["L0_ffn_w3"]),
        "w2_in": experts(arr["L0_ffn_w2"]),
        "cond_in": rows_by_chunk(arr["L0_c"].T),
        "wmod_in": rows_by_chunk(arr["L0_wmod"]),
        "const_in": const,
    }
    nc = bacc.Bacc("TRN2", target_bir_lowering=False, num_devices=1)
    aps = [nc.dram_tensor(n, a.shape, F32, kind="ExternalInput").ap() for n, a in feeds.items()]
    out = nc.dram_tensor("out", (TOKENS, D), F32, kind="ExternalOutput").ap()
    build(nc, *aps, out)
    r = run_bass_kernel_spmd(nc, [feeds], core_ids=[0])
    return r.results[0]["out"].reshape(BATCH, SEQ, D)
```

```python
from contextlib import ExitStack

import concourse.bass as bass
from concourse import mybir

P = 128
BATCH, SEQ, D, NSTATE = 4, 512, 256, 128
E, I, TOPK = 8, 512, 2
TOKENS = BATCH * SEQ
TILES = TOKENS // P
PB = SEQ // P
KD = D // P
KI = I // P
SLOT_TILES = TOKENS * TOPK // P + E - 1
WSTEP = KD * I
assert WSTEP == KI * D
EPS = 1e-5
JITTER2 = 0.02
FAR = -3.0e38

F32 = mybir.dt.float32
BF16 = mybir.dt.bfloat16
F16 = mybir.dt.float16
I32 = mybir.dt.int32
U32 = mybir.dt.uint32
ALU = mybir.AluOpType
ACT = mybir.ActivationFunctionType
AX_X = mybir.AxisListType.X

C_ID = 0
C_UP = C_ID + P
C_IOTA = C_UP + P
C_TOK = C_IOTA + P
C_TIE = C_TOK + 2 * TILES
C_TRASH = C_TIE + E
C_END = C_TRASH + 1


def build(nc, x_in, bT_in, c_in, dT_in, gw_in, w_in, cond_in, wmod_in, const_in, out):
    ctx = ExitStack()
    with ctx:
        def sb(name, cols, dt=F32):
            return ctx.enter_context(nc.sbuf_tensor(name, [P, cols], dt))

        def sem(name):
            return ctx.enter_context(nc.semaphore(name))

        h2_dram = nc.dram_tensor("h2_rows", (TOKENS, D), F32, kind="Internal").ap()
        moe_dram = nc.dram_tensor("moe_sum", (TOKENS + P, D), F32, kind="Internal").ap()
        mod_dram = nc.dram_tensor("mod_rows", (BATCH, 3 * D), F32, kind="Internal").ap()

        w = sb("experts", 3 * E * WSTEP)
        W1, W3, W2 = 0, E * WSTEP, 2 * E * WSTEP
        x = sb("x", TILES * D)
        wmod = sb("wmod", KD * 6 * D)
        const = sb("const", C_END)
        bT = sb("bT", KD * NSTATE)
        c_nat = sb("c_nat", KD * NSTATE)
        dT = sb("dT", KD)
        gw = sb("gw", KD * E)
        cond = sb("cond", KD * BATCH)
        cond_silu = sb("cond_silu", KD * BATCH)
        WC = KD * BATCH
        mod_col = sb("mod_col", 5 * WC)
        gate_tmp = sb("gate_tmp", 2 * WC)
        ga_d = sb("ga_d", WC)
        mod_row = sb("mod_row", 3 * D)
        row_tmp = sb("row_tmp", 2 * D)
        mod_all = sb("mod_all", BATCH * 3 * D)
        c_ga = sb("c_ga", BATCH * D)
        diag = sb("diag", BATCH * D)
        zeros = sb("zeros", D)
        stats = sb("stats", PB * 6)
        mean_var = sb("mean_var", PB * 2)
        var_eps = sb("var_eps", PB)
        rstd = sb("rstd", PB)
        stats2 = sb("stats2", PB * 6)
        mean_var2 = sb("mean_var2", PB * 2)
        var_eps2 = sb("var_eps2", PB)
        minus_mean2 = sb("minus_mean2", PB)
        rstd2 = sb("rstd2", PB)
        shift2 = sb("shift2", PB)
        minus_half = sb("minus_half", PB)
        work = sb("work", 4 * PB * D)
        xhat = work[:, 0:PB * D]
        xhat2 = work[:, PB * D:2 * PB * D]
        hT = work[:, 2 * PB * D:3 * PB * D]
        h2T = work[:, 3 * PB * D:4 * PB * D]
        c_scaled = xhat2
        stateT = sb("stateT", SEQ)
        h2 = sb("h2", PB * D)
        R = PB * E
        logit = sb("logit", 2 * R)
        logit_abs = sb("logit_abs", R)
        top = sb("top", 2 * PB)
        tie = sb("tie", R)
        tie_max = sb("tie_max", PB)
        pick = sb("pick", BATCH * 2 * R)
        below = sb("below", 2 * R)
        scale = sb("scale", R)
        keep = sb("keep", 2 * R)
        expo = sb("expo", 2 * R)
        expo_sum = sb("expo_sum", 2 * PB)
        gate = sb("gate", BATCH * 2 * PB)
        both = sb("both", R, BF16)
        before = sb("before", (TILES + 1) * E, BF16)
        upper_b = sb("upper_b", P, BF16)
        ones_b = sb("ones_b", P, BF16)
        rank_pick = sb("rank_pick", 2 * R)
        rank = sb("rank", 2 * PB)
        rank_i = sb("rank_i", 2 * PB, I32)
        lo_i = sb("lo_i", 2 * PB, I32)
        hi_i = sb("hi_i", 2 * PB, I32)
        lo_h = sb("lo_h", 2 * PB, F16)
        hi_part = sb("hi_part", BATCH * 2 * PB)
        NP = BATCH * 2 * PB
        lo_hot = sb("lo_hot", NP * P, F16)
        cnt_i = sb("cnt_i", E, I32)
        tiles_i = sb("tiles_i", E, I32)
        scan = [sb(f"scan{n}", 2 * E) for n in range(4)]
        first_tile = sb("first_tile", E)
        first_pick = sb("first_pick", NP * E)
        first_of = sb("first_of", NP)
        hi_h = sb("hi_h", NP, F16)
        gate_hi = sb("gate_hi", NP, F16)
        gate_lo = sb("gate_lo", NP, F16)
        gate_rest = sb("gate_rest", NP)
        iota_h = sb("iota_h", P, F16)
        tok_h = sb("tok_h", 2 * TILES, F16)
        past = sb("past", SLOT_TILES * E)
        expert_f = sb("expert_f", SLOT_TILES)
        expert_off = sb("expert_off", SLOT_TILES, I32)
        HV = 3 * SLOT_TILES
        hi_hot = sb("hi_hot", NP * SLOT_TILES, F16)
        hi_val = wmod[:, :].bitcast(F16)[:, 0:NP * HV]
        slot_tab = sb("slot_tab", HV)
        slot_gate = sb("slot_gate", SLOT_TILES)
        empty = sb("empty", SLOT_TILES)
        row_from = sb("row_from", SLOT_TILES, U32)
        row_to = sb("row_to", SLOT_TILES, U32)
        from_now = sb("from_now", 2, U32)
        to_now = sb("to_now", 1, U32)
        rows = [work[:, n * D:(n + 1) * D] for n in range(2)]
        rowsT = work[:, 2 * D:2 * D + KD * P]
        silu = work[:, 4 * D:4 * D + I]
        act_ = work[:, 6 * D:6 * D + I]
        actT = work[:, 8 * D:8 * D + KI * P]
        y_gated = work[:, 10 * D:11 * D]

        ident = const[:, C_ID:C_ID + P]

        bank = [ctx.enter_context(nc.psum_tensor(f"bank{n}", [P, 512], F32)) for n in range(8)]
        xhatT_ps = bank[0:2]
        state_ps = bank[2]
        attn_ps = bank[3:5]
        c_ga_ps = bank[3:5]
        h2T_ps = bank[5:7]
        mod_row_ps = bank[5:7]
        logit_ps = bank[7][:, 0:R]
        rank_ps = bank[7][:, R:2 * R]
        count_ps = bank[2][:, 0:E]
        mod_col_ps = bank[2]
        mod_col2_ps = bank[7]
        tab_ps = bank[3]
        up1_ps, up3_ps = bank[0], bank[1]
        rowsT_ps = bank[2]
        actT_ps = bank[5]
        y_ps = bank[4]

        const_loaded = sem("const_loaded")
        cond_loaded = sem("cond_loaded")
        x_first_loaded = sem("x_batch0_loaded")
        x_rest_loaded = sem("x_rest_loaded")
        small_loaded = sem("small_weights_loaded")
        wmod_loaded = sem("wmod_loaded")
        w_loaded = sem("expert_weights_loaded")
        zeros_set = sem("zeros_set")
        consts_set = sem("pool_constants_set")
        moe_zeroed = sem("moe_sum_zeroed")
        mod_stored = sem("mod_rows_stored")
        mod_spread = sem("mod_rows_spread")
        cond_done = sem("silu_of_cond_done")
        col_ready = sem("mod_col_psum_ready")
        col2_ready = sem("mod_col2_psum_ready")
        row_ready = sem("mod_row_psum_ready")
        modcol_done = sem("mod_col_done")
        modrow_done = sem("mod_row_done")
        c_scaled_ready = sem("c_scaled_ready")
        c_ga_ps_ready = sem("c_ga_psum_ready")
        c_ga_ready = sem("c_ga_ready")
        diag_ready = sem("diag_ready")
        var_ready = sem("var_eps_ready")
        rstd_ready = sem("rstd_ready")
        var2_ready = sem("var_eps2_ready")
        rstd2_ready = sem("rstd2_ready")
        shift2_ready = sem("shift2_ready")
        xhat_ready = sem("xhat_ready")
        xhatT_ready = sem("xhatT_psum_ready")
        hT_ready = sem("hT_ready")
        state_ps_ready = sem("state_psum_ready")
        state_ready = sem("state_ready")
        attn_ready = sem("attn_psum_ready")
        x1_ready = sem("x1_ready")
        xhat2_ready = sem("xhat2_ready")
        h2_scaled = sem("h2_scaled")
        h2_ready = sem("h2_ready")
        h2T_ps_ready = sem("h2T_psum_ready")
        h2T_ready = sem("h2T_ready")
        logits_ready = sem("logits_psum_ready")
        h2_stored = sem("h2_rows_stored")
        dve_done = sem("vector_step_done")
        below_ready = sem("distances_ready")
        expo_ready = sem("exponentials_ready")
        before_ready = sem("pair_counts_ready")
        rank_ready = sem("ranks_psum_ready")
        rank_read = sem("ranks_read")
        count_ready = sem("expert_totals_ready")
        hot_ready = sem("slot_one_hots_ready")
        table_ps_ready = sem("slot_table_psum_ready")
        table_ready = sem("slot_tables_ready")
        idx_ready = sem("row_indices_copied")
        rows_loaded = [sem(f"rows_gathered{n}") for n in range(2)]
        rowsT_ps_ready = sem("rowsT_psum_ready")
        rowsT_ready = sem("rowsT_ready")
        up1_ready = sem("up1_psum_ready")
        up3_ready = sem("up3_psum_ready")
        silu_ready = sem("silu_ready")
        act_ready = sem("act_ready")
        actT_ps_ready = sem("actT_psum_ready")
        actT_ready = sem("actT_ready")
        y_ready = sem("y_psum_ready")
        y_gated_ready = sem("y_gated_ready")
        y_added = sem("y_added_to_moe_sum")
        moe_loaded = [sem(f"moe_sum_loaded{b}") for b in range(BATCH)]
        out_ready = sem("out_ready")
        out_stored = sem("out_stored")

        block = ctx.enter_context(nc.Block())

        moe_sb = w
        LAST = SLOT_TILES - 1
        UNROLL = 4
        HEAD = 2 + (LAST - 2) % UNROLL
        assert HEAD % 2 == 0 and (LAST - HEAD) % UNROLL == 0

        @block.sync
        def _(sp):
            def x_rows(ap, b, n):
                return ap[b * SEQ:(b + n) * SEQ, :].rearrange("(j p) d -> p j d", p=P)

            def tiles(t, b, n):
                return t[:, b * PB * D:(b + n) * PB * D].rearrange("p (j d) -> p j d", d=D)

            sp.dma_start(cond[:, :], cond_in).then_inc(cond_loaded, 16)
            sp.dma_start(tiles(x, 0, 1), x_rows(x_in, 0, 1)).then_inc(x_first_loaded, 16)
            sp.dma_start(const[:, :], const_in).then_inc(const_loaded, 16)
            sp.dma_start(wmod[:, :], wmod_in).then_inc(wmod_loaded, 16)
            sp.dma_start(c_nat[:, :], c_in).then_inc(small_loaded, 16)
            sp.dma_start(bT[:, :], bT_in).then_inc(small_loaded, 16)
            sp.dma_start(dT[:, :], dT_in).then_inc(small_loaded, 16)
            sp.dma_start(gw[:, :], gw_in).then_inc(small_loaded, 16)
            sp.dma_start(tiles(x, 1, 3), x_rows(x_in, 1, 3)).then_inc(x_rest_loaded, 16)
            sp.wait_ge(modrow_done, 1)
            sp.dma_start(mod_dram, mod_row[0:BATCH, :]).then_inc(mod_stored, 16)
            sp.wait_ge(mod_stored, 16)
            sp.dma_start(mod_all[:, :], mod_dram.rearrange("(a b) c -> a (b c)", a=1).to_broadcast((P, BATCH * 3 * D)))\
                .then_inc(mod_spread, 16)
            sp.wait_ge(zeros_set, 1)
            part = 3 * E * WSTEP // BATCH
            with sp.Fori(0, BATCH) as b:
                sp.dma_start(w[:, bass.ds(b * part, part)], w_in[:, bass.ds(b * part, part)]).then_inc(w_loaded, 16)
                sp.wait_ge(h2_ready, b + 1)
                sp.dma_start(h2_dram[bass.ds(b * SEQ, SEQ), :].rearrange("(j p) d -> p j d", p=P),
                             h2[:, :].rearrange("p (j d) -> p j d", d=D)).then_inc(h2_stored, 16)
            sp.wait_ge(y_added, 16 * SLOT_TILES)
            for b in range(BATCH):
                sp.dma_start(tiles(moe_sb, b, 1), x_rows(moe_dram, b, 1)).then_inc(moe_loaded[b], 16)
            for b in range(BATCH):
                sp.wait_ge(out_ready, b + 1)
                sp.dma_start(x_rows(out, b, 1), tiles(x, b, 1)).then_inc(out_stored, 16)
            sp.wait_ge(out_stored, 16 * BATCH)

        @block.gpsimd
        def _(pool):
            pool.memset(zeros[:, :], 0.0).then_inc(zeros_set, 1)
            pool.memset(minus_half[:, :], -0.5).then_inc(consts_set, 1)
            pool.memset(ones_b[:, :], 1.0).then_inc(consts_set, 1)
            for n in range(4):
                pool.memset(scan[n][:, 0:E], 0.0).then_inc(consts_set, 1)
            pool.memset(before[:, 0:E], 0.0).then_inc(consts_set, 1)
            pool.wait_ge(consts_set, 7)

            def power1(b):
                pool.wait_ge(var_ready, b + 1)
                pool.tensor_tensor(rstd[:, :], var_eps[:, :], minus_half[:, :], ALU.pow).then_inc(rstd_ready, 1)

            def power2(b):
                pool.wait_ge(var2_ready, b + 1)
                pool.tensor_tensor(rstd2[:, :], var_eps2[:, :], minus_half[:, :], ALU.pow).then_inc(rstd2_ready, 1)
                pool.wait_ge(rstd2_ready, b + 1)
                pool.tensor_tensor(shift2[:, :], minus_mean2[:, :], rstd2[:, :], ALU.mult).then_inc(shift2_ready, 1)

            def modulate_h2(b):
                def row(m):
                    return mod_all[:, bass.ds(b * (3 * D) + m * D, D)].unsqueeze(1).to_broadcast((P, PB, D))

                h3 = h2[:, :].rearrange("p (j d) -> p j d", d=D)
                pool.wait_ge(xhat2_ready, PB * (b + 1))
                pool.tensor_tensor(h3, xhat2.rearrange("p (j d) -> p j d", d=D), row(1), ALU.mult).then_inc(h2_scaled, 1)
                pool.wait_ge(h2_scaled, b + 1)
                pool.tensor_tensor(h3, h3, row(0), ALU.add).then_inc(h2_ready, 1)

            power1(0)
            power1(1)
            pool.dma_start(moe_dram.rearrange("(j p) d -> p j d", p=P),
                           zeros[:, :].unsqueeze(1).to_broadcast((P, TILES + 1, D))).then_inc(moe_zeroed, 16)
            power2(0)
            pool.wait_ge(mod_spread, 16)
            modulate_h2(0)
            with pool.Fori(1, BATCH - 1) as b:
                power1(b + 1)
                power2(b)
                pool.wait_ge(h2_stored, 16 * b)
                modulate_h2(b)
            power2(BATCH - 1)
            pool.wait_ge(h2_stored, 16 * (BATCH - 1))
            modulate_h2(BATCH - 1)

            copies = pool.alloc_register("index_copies")

            def copy_index(now, table, s, count):
                pool.tensor_copy(now, table[:, bass.ds(s, 1)]).then_inc(idx_ready, 1)
                if count is None:
                    pool.reg_add(copies, copies, 1)
                    count = copies
                pool.wait_ge(moe_zeroed, 16)
                pool.wait_ge(idx_ready, count)

            def fetch(s, h, count=None):
                copy_index(from_now[:, h:h + 1], row_from, s, count)
                pool.indirect_dma_start(rows[h], None, h2_dram,
                                        bass.IndirectOffsetOnAxis(ap=from_now[:, h:h + 1], axis=0))\
                    .then_inc(rows_loaded[h], 16)

            def add_back(s, count=None):
                pool.wait_ge(y_gated_ready, s + 1)
                copy_index(to_now[:, :], row_to, s, count)
                pool.indirect_dma_start(moe_dram, bass.IndirectOffsetOnAxis(ap=to_now[:, :], axis=0), y_gated,
                                        None, compute_op=ALU.add).then_inc(y_added, 16)

            pool.wait_ge(table_ready, 1)
            pool.wait_ge(h2_stored, 16 * BATCH)
            fetch(0, 0, 1)
            fetch(1, 1, 2)
            done = 2
            for s in range(1, HEAD):
                pool.wait_ge(rowsT_ps_ready, s)
                fetch(s + 1, (s + 1) % 2, done + 1)
                if s >= 2:
                    pool.wait_ge(y_added, 16 * (s - 1))
                add_back(s - 1, done + 2)
                done += 2
            pool.reg_mov(copies, done)
            with pool.Fori(0, (LAST - HEAD) // UNROLL) as r:
                s0 = r * UNROLL + HEAD
                for u in range(UNROLL):
                    s = s0 + u
                    pool.wait_ge(rowsT_ps_ready, s)
                    fetch(s + 1, (u + 1) % 2)
                    pool.wait_ge(y_added, 16 * (s - 1))
                    add_back(s - 1)
            for s in (LAST - 1, LAST):
                pool.wait_ge(y_added, 16 * s)
                add_back(s, SLOT_TILES + 1 + s)

        @block.scalar
        def _(act):
            act.wait_ge(cond_loaded, 16)
            act.activation(cond_silu[:, :], cond[:, :], ACT.Silu).then_inc(cond_done, 1)

            def modulate(b):
                for k in range(KD):
                    act.wait_ge(xhatT_ready, KD * b + k + 1)
                    act.activation(hT[:, k * SEQ:(k + 1) * SEQ], xhatT_ps[k][:, :], ACT.Identity,
                                   bias=mod_col[:, bass.ds(b + k * BATCH, 1)],
                                   scale=mod_col[:, bass.ds(b + WC + k * BATCH, 1)]).then_inc(hT_ready, 1)

            def state(b):
                act.wait_ge(state_ps_ready, b + 1)
                act.activation(stateT[:, :], state_ps[:, :], ACT.Tanh).then_inc(state_ready, 1)

            def normalize2(b):
                act.wait_ge(shift2_ready, b + 1)
                for q in range(PB):
                    act.activation(xhat2[:, q * D:(q + 1) * D], x[:, bass.ds(b * (PB * D) + q * D, D)], ACT.Identity,
                                   bias=shift2[:, q:q + 1], scale=rstd2[:, q:q + 1]).then_inc(xhat2_ready, 1)

            def modulate2(b):
                for k in range(KD):
                    act.wait_ge(h2T_ps_ready, KD * b + k + 1)
                    act.activation(h2T[:, k * SEQ:(k + 1) * SEQ], h2T_ps[k][:, :], ACT.Identity,
                                   bias=mod_col[:, bass.ds(b + 3 * WC + k * BATCH, 1)],
                                   scale=mod_col[:, bass.ds(b + 4 * WC + k * BATCH, 1)]).then_inc(h2T_ready, 1)

            def exponentials(b):
                act.wait_ge(below_ready, 2 * (b + 1))
                act.activation(expo[:, :], below[:, :], ACT.Exp, scale=-1.0).then_inc(expo_ready, 1)

            act.wait_ge(modcol_done, 1)
            modulate(0)
            for n in range(2):
                act.wait_ge(c_ga_ps_ready, n + 1)
                act.activation(c_ga[:, n * 512:(n + 1) * 512], c_ga_ps[n][:, :], ACT.Copy).then_inc(c_ga_ready, 1)
            state(0)
            act.wait_ge(attn_ready, 2)
            modulate(1)
            state(1)
            act.wait_ge(modcol_done, 2)
            normalize2(0)
            modulate2(0)
            with act.Fori(1, BATCH - 1) as b:
                act.wait_ge(attn_ready, 2 * (b + 1))
                modulate(b + 1)
                state(b + 1)
                act.wait_ge(h2_ready, b)
                normalize2(b)
                exponentials(b - 1)
                act.wait_ge(logits_ready, b)
                modulate2(b)
            act.wait_ge(h2_ready, BATCH - 1)
            normalize2(BATCH - 1)
            exponentials(BATCH - 2)
            act.wait_ge(logits_ready, BATCH - 1)
            modulate2(BATCH - 1)
            exponentials(BATCH - 1)

            def copy_rowsT(s):
                act.wait_ge(rowsT_ps_ready, s + 1)
                act.activation(rowsT, rowsT_ps[:, 0:KD * P], ACT.Copy).then_inc(rowsT_ready, 1)

            copy_rowsT(0)

            def tile(s, more=True):
                act.wait_ge(up1_ready, s + 1)
                act.activation(silu, up1_ps[:, :], ACT.Silu).then_inc(silu_ready, 1)
                if more:
                    copy_rowsT(s + 1)
                act.wait_ge(actT_ps_ready, s + 1)
                act.activation(actT, actT_ps[:, :], ACT.Copy).then_inc(actT_ready, 1)

            for s in range(HEAD):
                tile(s)
            with act.Fori(0, (LAST - HEAD) // UNROLL) as r:
                s0 = r * UNROLL + HEAD
                for u in range(UNROLL):
                    tile(s0 + u)
            tile(LAST, False)

        @block.tensor
        def _(pe):
            def transpose_xhat(b):
                pe.wait_ge(xhat_ready, b + 1)
                for k in range(KD):
                    for q in range(PB):
                        last = pe.transpose(xhatT_ps[k][:, q * P:(q + 1) * P],
                                            xhat[:, q * D + k * P:q * D + (k + 1) * P], ident)
                    last.then_inc(xhatT_ready, 1)

            def mod_columns(ps, ms):
                for n, m in enumerate(ms):
                    for c in range(KD):
                        for k in range(KD):
                            col = k * 6 * D + m * D + c * P
                            last = pe.matmul(ps[:, n * WC + c * BATCH:n * WC + (c + 1) * BATCH], wmod[:, col:col + P],
                                             cond_silu[:, k * BATCH:(k + 1) * BATCH],
                                             start=(k == 0), stop=(k == KD - 1))
                return last

            def state_in(b):
                for k in range(KD):
                    pe.wait_ge(hT_ready, KD * b + k + 1)
                    last = pe.matmul(state_ps[:, :], bT[:, k * NSTATE:(k + 1) * NSTATE], hT[:, k * SEQ:(k + 1) * SEQ],
                                     start=(k == 0), stop=(k == KD - 1))
                last.then_inc(state_ps_ready, 1)

            def attn(b):
                pe.wait_ge(state_ready, b + 1)
                for q in range(PB):
                    o = attn_ps[q // 2]
                    c0 = (q % 2) * D
                    pe.matmul(o[:, c0:c0 + D], stateT[:, q * P:(q + 1) * P], c_ga[:, bass.ds(b * D, D)],
                              start=True, stop=False)
                    for k in range(KD):
                        last = pe.matmul(o[:, c0 + k * P:c0 + (k + 1) * P], hT[:, k * SEQ + q * P:k * SEQ + (q + 1) * P],
                                         diag[:, bass.ds(b * D + k * P, P)], start=False, stop=(k == KD - 1))
                    if q % 2:
                        last.then_inc(attn_ready, 1)

            def transpose_xhat2(b):
                pe.wait_ge(xhat2_ready, PB * (b + 1))
                for k in range(KD):
                    for q in range(PB):
                        last = pe.transpose(h2T_ps[k][:, q * P:(q + 1) * P],
                                            xhat2[:, q * D + k * P:q * D + (k + 1) * P], ident)
                    last.then_inc(h2T_ps_ready, 1)

            def logits(b):
                pe.wait_ge(h2T_ready, KD * (b + 1))
                for q in range(PB):
                    for k in range(KD):
                        last = pe.matmul(logit_ps[:, q * E:(q + 1) * E],
                                         h2T[:, k * SEQ + q * P:k * SEQ + (q + 1) * P], gw[:, k * E:(k + 1) * E],
                                         start=(k == 0), stop=(k == KD - 1))
                last.then_inc(logits_ready, 1)

            def ranks(b):
                pe.wait_ge(before_ready, b + 1)
                pe.matmul(rank_ps, upper_b[:, :], both[:, :], start=True, stop=False)
                last = pe.matmul(rank_ps, ones_b[:, :], before[:, bass.ds(b * R, R)], start=False, stop=True)
                last.then_inc(rank_ready, 1)

            pe.wait_ge(const_loaded, 16)
            transpose_xhat(0)
            pe.wait_ge(cond_done, 1)
            pe.wait_ge(wmod_loaded, 16)
            mod_columns(mod_col_ps, (0, 1, 2)).then_inc(col_ready, 1)
            mod_columns(mod_col2_ps, (3, 4)).then_inc(col2_ready, 1)
            pe.wait_ge(small_loaded, 64)
            pe.wait_ge(modcol_done, 1)
            state_in(0)
            for n in range(2):
                pe.wait_ge(c_scaled_ready, n + 1)
                for i in range(4):
                    last = pe.transpose(c_ga_ps[n][:, i * P:(i + 1) * P], c_scaled[:, (4 * n + i) * P:(4 * n + i + 1) * P],
                                        ident)
                last.then_inc(c_ga_ps_ready, 1)
            for n, (m, width) in enumerate(((3, 512), (5, 256))):
                for k in range(KD):
                    last = pe.matmul(mod_row_ps[n][0:BATCH, 0:width], cond_silu[:, k * BATCH:(k + 1) * BATCH],
                                     wmod[:, k * 6 * D + m * D:k * 6 * D + m * D + width],
                                     start=(k == 0), stop=(k == KD - 1))
            last.then_inc(row_ready, 1)
            pe.wait_ge(c_ga_ready, 2)
            pe.wait_ge(diag_ready, 1)
            attn(0)
            transpose_xhat(1)
            state_in(1)
            pe.wait_ge(modrow_done, 1)
            transpose_xhat2(0)
            pe.wait_ge(modcol_done, 2)
            logits(0)
            with pe.Fori(1, BATCH - 1) as b:
                pe.wait_ge(x1_ready, 2 * b)
                attn(b)
                transpose_xhat(b + 1)
                state_in(b + 1)
                transpose_xhat2(b)
                ranks(b - 1)
                pe.wait_ge(rank_read, b)
                logits(b)
            pe.wait_ge(x1_ready, 2 * (BATCH - 1))
            attn(BATCH - 1)
            transpose_xhat2(BATCH - 1)
            ranks(BATCH - 2)
            pe.wait_ge(rank_read, BATCH - 1)
            logits(BATCH - 1)
            ranks(BATCH - 1)
            pe.matmul(count_ps, ones_b[:, :], before[:, TILES * E:(TILES + 1) * E], start=True, stop=True)\
                .then_inc(count_ready, 1)
            for g in range(2):
                pe.wait_ge(hot_ready, g + 1)
                for n in range(g * NP // 2, (g + 1) * NP // 2):
                    last = pe.matmul(tab_ps[:, 0:HV], lo_hot[:, n * P:(n + 1) * P], hi_val[:, n * HV:(n + 1) * HV],
                                     start=(n == 0), stop=(n == NP - 1))
            last.then_inc(table_ps_ready, 1)

            def transpose_rows(s, h, count):
                pe.wait_ge(rows_loaded[h], count)
                for k in range(KD):
                    last = pe.transpose(rowsT_ps[:, k * P:(k + 1) * P], rows[h][:, k * P:(k + 1) * P], ident)
                last.then_inc(rowsT_ps_ready, 1)

            def up(s, off):
                pe.wait_ge(rowsT_ready, s + 1)
                for m, ps, done in ((W1, up1_ps, up1_ready), (W3, up3_ps, up3_ready)):
                    for k in range(KD):
                        last = pe.matmul(ps[:, :], rowsT[:, k * P:(k + 1) * P], w[:, bass.ds(off + m + k * I, I)],
                                         start=(k == 0), stop=(k == KD - 1))
                    last.then_inc(done, 1)

            def down(s, off):
                pe.wait_ge(actT_ready, s + 1)
                for k in range(KI):
                    last = pe.matmul(y_ps[:, 0:D], actT[:, k * P:(k + 1) * P], w[:, bass.ds(off + W2 + k * D, D)],
                                     start=(k == 0), stop=(k == KI - 1))
                last.then_inc(y_ready, 1)

            def transpose_act(s):
                pe.wait_ge(act_ready, s + 1)
                for k in range(KI):
                    last = pe.transpose(actT_ps[:, k * P:(k + 1) * P], act_[:, k * P:(k + 1) * P], ident)
                last.then_inc(actT_ps_ready, 1)

            def weight_column(s):
                return pe.value_load(expert_off[0:1, bass.ds(s, 1)], min_val=0, max_val=(E - 1) * WSTEP)

            pe.wait_ge(w_loaded, 16 * BATCH)
            pe.wait_ge(table_ready, 1)
            transpose_rows(0, 0, 16)
            before_off = None
            for s in range(HEAD):
                off = weight_column(s)
                up(s, off)
                transpose_rows(s + 1, (s + 1) % 2, 16 * ((s + 1) // 2 + 1))
                if s >= 2:
                    pe.wait_ge(y_gated_ready, s - 1)
                if s >= 1:
                    down(s - 1, before_off)
                transpose_act(s)
                before_off = off
            with pe.Fori(0, (LAST - HEAD) // UNROLL) as r:
                s0 = r * UNROLL + HEAD
                before_off = weight_column(s0 - 1)
                for u in range(UNROLL):
                    s = s0 + u
                    off = weight_column(s)
                    up(s, off)
                    transpose_rows(s + 1, (u + 1) % 2, 8 * s0 + 16 * ((u + 1) // 2 + 1))
                    pe.wait_ge(y_gated_ready, s - 1)
                    down(s - 1, before_off)
                    transpose_act(s)
                    before_off = off
            before_off, off = weight_column(LAST - 1), weight_column(LAST)
            up(LAST, off)
            pe.wait_ge(y_gated_ready, LAST - 1)
            down(LAST - 1, before_off)
            transpose_act(LAST)
            pe.wait_ge(y_gated_ready, LAST)
            down(LAST, off)

        @block.vector
        def _(dve):
            steps = [0]
            step_count = dve.alloc_register("vector_steps")
            x1_count = dve.alloc_register("x1_parts")

            def link(ins, looped=False):
                ins.then_inc(dve_done, 1)
                steps[0] += 1
                if looped:
                    dve.reg_add(step_count, step_count, 1)
                    dve.wait_ge(x_first_loaded, 16)
                    dve.wait_ge(dve_done, step_count)
                else:
                    dve.wait_ge(dve_done, steps[0])

            def norm_stats(b, lp, st, mv):
                for q in range(PB):
                    last = dve.bn_stats(st[:, q * 6:(q + 1) * 6], x[:, bass.ds(b * (PB * D) + q * D, D)])
                link(last, lp)
                for q in range(PB):
                    last = dve.bn_aggr(mv[:, q * 2:(q + 1) * 2], st[:, q * 6:(q + 1) * 6])
                link(last, lp)

            def front(b, lp=False):
                norm_stats(b, lp, stats, mean_var)
                dve.tensor_scalar(var_eps[:, :], mean_var[:, 1:2 * PB:2], EPS, None, ALU.add).then_inc(var_ready, 1)
                dve.wait_ge(rstd_ready, b + 1)
                for q in range(PB):
                    last = dve.tensor_scalar(xhat[:, q * D:(q + 1) * D], x[:, bass.ds(b * (PB * D) + q * D, D)],
                                             mean_var[:, 2 * q:2 * q + 1], rstd[:, q:q + 1],
                                             ALU.subtract, ALU.mult)
                last.then_inc(xhat_ready, 1)

            def residual(b, lp=False):
                for g in range(2):
                    dve.wait_ge(attn_ready, 2 * b + g + 1)
                    xs = x[:, bass.ds(b * (PB * D) + g * 2 * D, 2 * D)]
                    dve.tensor_tensor(xs, attn_ps[g][:, :], xs, ALU.add).then_inc(x1_ready, 1)
                if lp:
                    dve.reg_add(x1_count, x1_count, 2)
                    dve.wait_ge(x_first_loaded, 16)
                    dve.wait_ge(x1_ready, x1_count)
                else:
                    dve.wait_ge(x1_ready, 2 * b + 2)
                norm_stats(b, lp, stats2, mean_var2)
                dve.tensor_scalar(minus_mean2[:, :], mean_var2[:, 0:2 * PB:2], -1.0, None, ALU.mult)
                dve.tensor_scalar(var_eps2[:, :], mean_var2[:, 1:2 * PB:2], EPS, None, ALU.add).then_inc(var2_ready, 1)

            def je(ap, n=PB):
                return ap.rearrange("p (j e) -> p j e", e=E)

            def over_e(ap, n=PB):
                return ap.unsqueeze(2).to_broadcast((P, n, E))

            tie_w = const[:, C_TIE:C_TIE + E].unsqueeze(1).to_broadcast((P, PB, E))

            def choose(b, lp=False):
                dve.wait_ge(logits_ready, b + 1)
                link(dve.tensor_copy(logit[:, 0:R], logit_ps), lp)
                link(dve.scalar_tensor_tensor(logit_abs[:, :], logit[:, 0:R], -1.0, logit[:, 0:R], ALU.mult, ALU.max), lp)
                for c in range(TOPK):
                    score = logit[:, c * R:(c + 1) * R]
                    tops = top[:, c * PB:(c + 1) * PB]
                    far = below[:, c * R:(c + 1) * R]
                    picks = pick[:, bass.ds(b * (2 * R) + c * R, R)]
                    link(dve.tensor_reduce(tops, je(score), AX_X, ALU.max), lp)
                    dve.tensor_tensor(je(far), over_e(tops), je(score), ALU.subtract).then_inc(below_ready, 1)
                    dve.tensor_tensor(je(scale[:, :]), je(logit_abs[:, :]), over_e(tops), ALU.max)
                    link(dve.tensor_tensor(je(picks), je(score), over_e(tops), ALU.is_equal), lp)
                    dve.scalar_tensor_tensor(keep[:, c * R:(c + 1) * R], scale[:, :], JITTER2, far, ALU.mult, ALU.is_ge)
                    link(dve.tensor_tensor(je(tie[:, :]), je(picks), tie_w, ALU.mult), lp)
                    link(dve.tensor_reduce(tie_max[:, :], je(tie[:, :]), AX_X, ALU.max), lp)
                    link(dve.tensor_tensor(je(picks), je(tie[:, :]), over_e(tie_max[:, :]), ALU.is_equal), lp)
                    if c == 0:
                        link(dve.scalar_tensor_tensor(logit[:, R:2 * R], picks, FAR, score, ALU.mult, ALU.add), lp)
                link(dve.tensor_tensor(both[:, :], pick[:, bass.ds(b * (2 * R), R)],
                                       pick[:, bass.ds(b * (2 * R) + R, R)], ALU.add), lp)
                for q in range(PB):
                    now = before[:, bass.ds(b * R + q * E, E)]
                    last = dve.tensor_tensor(before[:, bass.ds(b * R + (q + 1) * E, E)], now,
                                             both[:, q * E:(q + 1) * E], ALU.add)
                    if q < PB - 1:
                        link(last, lp)
                last.then_inc(before_ready, 1)
                dve.wait_ge(expo_ready, b + 1)
                link(dve.tensor_tensor(keep[:, :], keep[:, :], expo[:, :], ALU.mult), lp)
                link(dve.tensor_reduce(expo_sum[:, :], je(keep[:, :]), AX_X, ALU.add), lp)
                link(dve.reciprocal(gate[:, bass.ds(b * (2 * PB), 2 * PB)], expo_sum[:, :]), lp)

            def place(b, lp=False):
                dve.wait_ge(rank_ready, b + 1)
                link(dve.tensor_tensor(rank_pick[:, :].rearrange("p (c r) -> p c r", r=R),
                                       pick[:, bass.ds(b * (2 * R), 2 * R)].rearrange("p (c r) -> p c r", r=R),
                                       rank_ps.unsqueeze(1).to_broadcast((P, 2, R)), ALU.mult), lp)
                link(dve.tensor_reduce(rank[:, :], je(rank_pick[:, :]), AX_X, ALU.add), lp)
                dve.tensor_copy(rank_i[:, :], rank[:, :]).then_inc(rank_read, 1)
                dve.wait_ge(rank_read, b + 1)
                dve.tensor_scalar(lo_i[:, :], rank_i[:, :], P - 1, None, ALU.bitwise_and)
                link(dve.tensor_scalar(hi_i[:, :], rank_i[:, :], 7, None, ALU.arith_shift_right), lp)
                link(dve.tensor_copy(lo_h[:, :], lo_i[:, :]), lp)
                dve.tensor_copy(hi_part[:, bass.ds(b * (2 * PB), 2 * PB)], hi_i[:, :])
                link(dve.tensor_tensor(lo_hot[:, bass.ds(b * (2 * PB * P), 2 * PB * P)].rearrange("p (n l) -> p n l", l=P),
                                       iota_h[:, :].unsqueeze(1).to_broadcast((P, 2 * PB, P)),
                                       lo_h[:, :].unsqueeze(2).to_broadcast((P, 2 * PB, P)), ALU.is_equal), lp)

            def clamp_gate(out_, in_, t_sign, t_abs):
                dve.tensor_scalar(t_sign, in_, 0.0, 2.0, ALU.is_ge, ALU.mult)
                link(dve.tensor_copy(out_, in_))
                link(dve.scalar_tensor_tensor(t_abs, out_, -1.0, out_, ALU.mult, ALU.max))
                link(dve.tensor_scalar(t_abs, t_abs, 0.25, None, ALU.max))
                return dve.scalar_tensor_tensor(out_, t_sign, -1.0, t_abs, ALU.add, ALU.mult)

            dve.wait_ge(x_first_loaded, 16)
            front(0)
            dve.wait_ge(const_loaded, 16)
            dve.tensor_copy(upper_b[:, :], const[:, C_UP:C_UP + P])
            dve.tensor_copy(tok_h[:, :], const[:, C_TOK:C_TOK + 2 * TILES])
            dve.tensor_copy(iota_h[:, :], const[:, C_IOTA:C_IOTA + P])

            dve.wait_ge(col_ready, 1)
            dve.tensor_scalar(mod_col[:, WC:2 * WC], mod_col_ps[:, WC:2 * WC], 1.0, None, ALU.add)
            dve.tensor_copy(mod_col[:, 0:WC], mod_col_ps[:, 0:WC])
            dve.tensor_copy(mod_col[:, 2 * WC:3 * WC], mod_col_ps[:, 2 * WC:3 * WC]).then_inc(modcol_done, 1)
            dve.wait_ge(modcol_done, 1)
            ga = mod_col[:, 2 * WC:3 * WC]
            link(clamp_gate(ga, ga, gate_tmp[:, 0:WC], gate_tmp[:, WC:2 * WC]))
            dve.wait_ge(small_loaded, 64)
            for b in range(BATCH):
                for k in range(KD):
                    last = dve.tensor_scalar(c_scaled[:, (b * KD + k) * P:(b * KD + k + 1) * P],
                                             c_nat[:, k * P:(k + 1) * P],
                                             mod_col[:, 2 * WC + k * BATCH + b:2 * WC + k * BATCH + b + 1], None, ALU.mult)
                if b % 2:
                    last.then_inc(c_scaled_ready, 1)
            link(dve.tensor_tensor(ga_d[:, :].rearrange("p (k b) -> p k b", b=BATCH),
                                   ga.rearrange("p (k b) -> p k b", b=BATCH),
                                   dT[:, :].unsqueeze(2).to_broadcast((P, KD, BATCH)), ALU.mult))
            for b in range(BATCH):
                for k in range(KD):
                    last = dve.tensor_scalar(diag[:, b * D + k * P:b * D + (k + 1) * P], ident,
                                             ga_d[:, k * BATCH + b:k * BATCH + b + 1], None, ALU.mult)
            last.then_inc(diag_ready, 1)
            dve.wait_ge(col2_ready, 1)
            dve.tensor_copy(mod_col[:, 3 * WC:4 * WC], mod_col2_ps[:, 0:WC])
            dve.tensor_scalar(mod_col[:, 4 * WC:5 * WC], mod_col2_ps[:, WC:2 * WC], 1.0, None, ALU.add)\
                .then_inc(modcol_done, 1)
            dve.wait_ge(row_ready, 1)
            g0, g1 = mod_row_ps[0], mod_row_ps[1]
            dve.tensor_copy(mod_row[0:BATCH, 0:D], g0[0:BATCH, 0:D])
            dve.tensor_scalar(mod_row[0:BATCH, D:2 * D], g0[0:BATCH, D:2 * D], 1.0, None, ALU.add)
            clamp_gate(mod_row[0:BATCH, 2 * D:3 * D], g1[0:BATCH, 0:D], row_tmp[0:BATCH, 0:D],
                       row_tmp[0:BATCH, D:2 * D]).then_inc(modrow_done, 1)
            dve.wait_ge(x_rest_loaded, 16)
            dve.wait_ge(xhatT_ready, KD)
            front(1)
            residual(0)
            at = steps[0]
            dve.reg_mov(step_count, at)
            dve.reg_mov(x1_count, 2)
            with dve.Fori(1, BATCH - 1) as b:
                dve.wait_ge(x_rest_loaded, 16)
                dve.wait_ge(xhatT_ready, KD * b + KD)
                front(b + 1, True)
                residual(b, True)
                choose(b - 1, True)
                place(b - 1, True)
            steps[0] = at + (BATCH - 2) * (steps[0] - at)
            residual(BATCH - 1)
            choose(BATCH - 2)
            place(BATCH - 2)
            dve.wait_ge(expo_ready, BATCH - 1)
            choose(BATCH - 1)
            place(BATCH - 1)

            dve.wait_ge(count_ready, 1)
            dve.wait_ge(consts_set, 7)
            link(dve.tensor_scalar(cnt_i[:, :], count_ps, float(P - 1), None, ALU.add))
            link(dve.tensor_scalar(tiles_i[:, :], cnt_i[:, :], 7, None, ALU.arith_shift_right))
            link(dve.tensor_copy(scan[0][:, E:2 * E], tiles_i[:, :]))
            for n, d in enumerate((1, 2, 4)):
                link(dve.tensor_tensor(scan[n + 1][:, E:2 * E], scan[n][:, E:2 * E], scan[n][:, E - d:2 * E - d],
                                       ALU.add))
            end_tile = scan[3][:, E:2 * E]
            link(dve.tensor_tensor(first_tile[:, :], end_tile, scan[0][:, E:2 * E], ALU.subtract))
            link(dve.tensor_tensor(je(first_pick[:, :]), je(pick[:, :]),
                                   first_tile[:, :].unsqueeze(1).to_broadcast((P, NP, E)), ALU.mult))
            link(dve.tensor_reduce(first_of[:, :], je(first_pick[:, :]), AX_X, ALU.add))
            link(dve.tensor_tensor(hi_h[:, :], first_of[:, :], hi_part[:, :], ALU.add))
            link(dve.tensor_copy(gate_hi[:, :], gate[:, :]))
            link(dve.tensor_tensor(gate_rest[:, :], gate[:, :], gate_hi[:, :], ALU.subtract))
            link(dve.tensor_scalar(gate_lo[:, :], gate_rest[:, :], 2048.0, None, ALU.mult))
            half = NP // 2

            def by_tile(ap, g):
                return ap[:, g * half:(g + 1) * half].unsqueeze(2).to_broadcast((P, half, SLOT_TILES))

            for g in range(2):
                hots = hi_hot[:, g * half * SLOT_TILES:(g + 1) * half * SLOT_TILES]\
                    .rearrange("p (n s) -> p n s", s=SLOT_TILES)
                vals = hi_val[:, g * half * HV:(g + 1) * half * HV].rearrange("p (n v) -> p n v", v=HV)
                link(dve.tensor_tensor(hots, iota_h[:, 0:SLOT_TILES].unsqueeze(1).to_broadcast((P, half, SLOT_TILES)),
                                       by_tile(hi_h, g), ALU.is_equal))
                for m, val in enumerate((tok_h, gate_hi, gate_lo)):
                    last = dve.tensor_tensor(vals[:, :, m * SLOT_TILES:(m + 1) * SLOT_TILES], hots, by_tile(val, g),
                                             ALU.mult)
                last.then_inc(hot_ready, 1)
            iota = const[:, C_IOTA:C_IOTA + P]
            link(dve.tensor_tensor(past[0:1, :].rearrange("p (s e) -> p s e", e=E),
                                   iota[0:1, 0:SLOT_TILES].unsqueeze(2).to_broadcast((1, SLOT_TILES, E)),
                                   end_tile[0:1, :].unsqueeze(1).to_broadcast((1, SLOT_TILES, E)), ALU.is_ge))
            link(dve.tensor_reduce(expert_f[0:1, :], past[0:1, :].rearrange("p (s e) -> p s e", e=E), AX_X, ALU.add))
            dve.tensor_scalar(expert_off[0:1, :], expert_f[0:1, :], float(E - 1), float(WSTEP), ALU.min, ALU.mult)
            dve.wait_ge(table_ps_ready, 1)
            link(dve.tensor_copy(slot_tab[:, :], tab_ps[:, 0:HV]))
            token1 = slot_tab[:, 0:SLOT_TILES]
            dve.tensor_scalar(row_from[:, :], token1, -1.0, 0.0, ALU.add, ALU.max)
            link(dve.tensor_scalar(empty[:, :], token1, 0.0, const[:, C_TRASH:C_TRASH + 1], ALU.is_equal, ALU.mult))
            dve.scalar_tensor_tensor(row_to[:, :], token1, -1.0, empty[:, :], ALU.add, ALU.add)\
                .then_inc(table_ready, 1)
            link(dve.scalar_tensor_tensor(slot_gate[:, :], slot_tab[:, 2 * SLOT_TILES:3 * SLOT_TILES], 1.0 / 2048.0,
                                          slot_tab[:, SLOT_TILES:2 * SLOT_TILES], ALU.mult, ALU.add))

            def gate_up(s):
                dve.wait_ge(silu_ready, s + 1)
                dve.wait_ge(up3_ready, s + 1)
                dve.tensor_tensor(act_, silu, up3_ps[:, :], ALU.mult).then_inc(act_ready, 1)

            def gate_y(s, wait_added=True):
                dve.wait_ge(y_ready, s + 1)
                if wait_added:
                    dve.wait_ge(y_added, 16 * s)
                dve.tensor_scalar(y_gated, y_ps[:, 0:D], slot_gate[:, bass.ds(s, 1)], None,
                                  ALU.mult).then_inc(y_gated_ready, 1)

            gate_up(0)
            gate_up(1)
            gate_y(0, False)
            for s in range(2, HEAD):
                gate_up(s)
                gate_y(s - 1)
            with dve.Fori(0, (LAST - HEAD) // UNROLL) as r:
                s0 = r * UNROLL + HEAD
                for u in range(UNROLL):
                    gate_up(s0 + u)
                    gate_y(s0 + u - 1)
            gate_up(LAST)
            gate_y(LAST - 1)
            gate_y(LAST)

            for b in range(BATCH):
                dve.wait_ge(moe_loaded[b], 16)
                m = moe_sb[:, b * PB * D:(b + 1) * PB * D]
                m3 = m.rearrange("p (j d) -> p j d", d=D)
                gb = mod_all[:, b * 3 * D + 2 * D:(b + 1) * 3 * D].unsqueeze(1).to_broadcast((P, PB, D))
                link(dve.tensor_tensor(m3, m3, gb, ALU.mult))
                xs = x[:, b * PB * D:(b + 1) * PB * D]
                dve.tensor_tensor(xs, xs, m, ALU.add).then_inc(out_ready, 1)


def kernel(**inputs):
    import numpy as np
    import concourse.bacc as bacc
    from concourse.bass_utils import run_bass_kernel_spmd

    def rows_by_chunk(a):
        c = a.shape[0] // P
        return np.ascontiguousarray(a.reshape(c, P, -1).transpose(1, 0, 2).reshape(P, -1))

    def experts(a):
        t = a.transpose(0, 2, 1)
        e, n, m = t.shape
        return np.ascontiguousarray(t.reshape(e, n // P, P, m).transpose(2, 0, 1, 3).reshape(P, -1))

    arr = {k: np.asarray(v) for k, v in inputs.items()}
    const = np.zeros((P, C_END), np.float32)
    const[:, C_ID:C_ID + P] = np.eye(P)
    const[:, C_UP:C_UP + P] = np.triu(np.ones((P, P)), 1)
    const[:, C_IOTA:C_IOTA + P] = np.arange(P)
    tile_of = (PB * np.arange(BATCH)[:, None, None] + np.zeros((TOPK, 1), int) + np.arange(PB)).ravel()
    const[:, C_TOK:C_TOK + 2 * TILES] = 1 + np.arange(P)[:, None] + P * tile_of
    const[:, C_TIE:C_TIE + E] = E - np.arange(E)
    const[:, C_TRASH] = TOKENS + 1 + np.arange(P)
    feeds = {
        "x_in": np.ascontiguousarray(arr["L0_attn_x"].reshape(TOKENS, D)),
        "bT_in": rows_by_chunk(arr["L0_attn_B"].T),
        "c_in": rows_by_chunk(arr["L0_attn_C"]),
        "dT_in": rows_by_chunk(arr["L0_attn_D"].reshape(D, 1)),
        "gw_in": rows_by_chunk(arr["L0_ffn_gate_w"].T),
        "w_in": np.concatenate([experts(arr["L0_ffn_" + n]) for n in ("w1", "w3", "w2")], axis=1),
        "cond_in": rows_by_chunk(arr["L0_c"].T),
        "wmod_in": rows_by_chunk(arr["L0_wmod"]),
        "const_in": const,
    }
    nc = bacc.Bacc("TRN2", target_bir_lowering=False, num_devices=1)
    aps = [nc.dram_tensor(n, a.shape, F32, kind="ExternalInput").ap() for n, a in feeds.items()]
    out = nc.dram_tensor("out", (TOKENS, D), F32, kind="ExternalOutput").ap()
    build(nc, *aps, out)
    r = run_bass_kernel_spmd(nc, [feeds], core_ids=[0])
    return r.results[0]["out"].reshape(BATCH, SEQ, D)
```

```python
from contextlib import ExitStack

import concourse.bass as bass
from concourse import mybir

P = 128
BATCH, SEQ, D, NSTATE = 4, 512, 256, 128
E, I, TOPK = 8, 512, 2
TOKENS = BATCH * SEQ
TILES = TOKENS // P
PB = SEQ // P
KD = D // P
KI = I // P
SLOT_TILES = TOKENS * TOPK // P + E - 1
ALWAYS = TOKENS * TOPK // P + E // 2
W3 = KD * I
W2 = 2 * W3
WSTEP = W2 + KI * D
MROW = 3 * D
PIECES = 3
GROUPS = 4
ROWS = 4
EPS = 1e-5
JITTER2 = 0.02
FAR = -3.0e38

F32 = mybir.dt.float32
BF16 = mybir.dt.bfloat16
F16 = mybir.dt.float16
I32 = mybir.dt.int32
U32 = mybir.dt.uint32
ALU = mybir.AluOpType
ACT = mybir.ActivationFunctionType
AX_X = mybir.AxisListType.X

C_ID = 0
C_UP = C_ID + P
C_IOTA = C_UP + P
C_TOK = C_IOTA + P
C_TIE = C_TOK + 2 * TILES
C_TRASH = C_TIE + E
C_BEFORE = C_TRASH + 1
C_END = C_BEFORE + E * E


def build(nc, x_in, bT_in, c_in, dT_in, gw_in, w_in, cond_in, wmod_in, const_in, out):
    ctx = ExitStack()
    with ctx:
        def sb(name, cols, dt=F32):
            return ctx.enter_context(nc.sbuf_tensor(name, [P, cols], dt))

        def sem(name):
            return ctx.enter_context(nc.semaphore(name))

        h2_dram = nc.dram_tensor("h2_gb_rows", (TOKENS, 2 * D), F32, kind="Internal").ap()
        mod_dram = nc.dram_tensor("mod_rows", (BATCH, 3 * D), F32, kind="Internal").ap()

        w = sb("experts", E * WSTEP)
        x = sb("x", TILES * D)
        wmod = sb("wmod", 2 * KD * MROW)
        const = sb("const", C_END)
        bT = sb("bT", KD * NSTATE)
        c_nat = sb("c_nat", KD * NSTATE)
        dT = sb("dT", KD)
        gw = sb("gw", KD * E)
        cond = sb("cond", KD * BATCH)
        cond_silu = sb("cond_silu", KD * BATCH)
        WC = KD * BATCH
        mod_col = sb("mod_col", 5 * WC)
        gate_tmp = sb("gate_tmp", 2 * WC)
        ga_d = sb("ga_d", WC)
        mod_row = sb("mod_row", 2 * MROW)
        row_tmp = sb("row_tmp", 2 * D)
        mod_all = sb("mod_all", BATCH * 3 * D)
        attn_w = sb("attn_w", 2 * BATCH * D)
        c_ga = attn_w[:, 0:BATCH * D]
        diag = attn_w[:, BATCH * D:]
        stats = sb("stats", PB * 6)
        mean_var = sb("mean_var", PB * 2)
        var_eps = sb("var_eps", PB)
        rstd = sb("rstd", PB)
        stats2 = sb("stats2", PB * 6)
        mean_var2 = sb("mean_var2", PB * 2)
        var_eps2 = sb("var_eps2", PB)
        minus_mean2 = sb("minus_mean2", PB)
        rstd2 = sb("rstd2", PB)
        shift2 = sb("shift2", PB)
        minus_half = sb("minus_half", PB)
        work = sb("work", 4 * PB * D)
        xhat = work[:, 0:PB * D]
        xhat2 = [work[:, PB * D:2 * PB * D], sb("xhat2_odd", PB * D)]
        hT = work[:, 2 * PB * D:3 * PB * D]
        h2T = work[:, 3 * PB * D:4 * PB * D]
        c_scaled = xhat2[0]
        stateT = sb("stateT", SEQ)
        assert SEQ >= 2 * D and ROWS % 2 == 0
        h2 = sb("h2", 2 * PB * D)
        R = PB * E
        TE = TILES * E
        NP = TOPK * TILES
        logit = sb("logit", 2 * TE)
        logit_abs = sb("logit_abs", TE)
        top = sb("top", NP)
        tie = sb("tie", TE)
        tie_max = sb("tie_max", TILES)
        pick = sb("pick", 2 * TE)
        below = sb("below", 2 * TE)
        scale = sb("scale", 2 * TE)
        keep = sb("keep", 2 * TE)
        expo = sb("expo", 2 * TE)
        expo_sum = sb("expo_sum", NP)
        gate = sb("gate", NP)
        both = sb("both", TE, BF16)
        upper_b = sb("upper_b", P, BF16)
        ones_b = sb("ones_b", P, BF16)
        slot_of = sb("slot_of", TE)
        slot_pick = sb("slot_pick", 2 * TE)
        slot = sb("slot", NP)
        slot_i = sb("slot_i", NP, I32)
        lo_i = sb("lo_i", NP, I32)
        hi_i = sb("hi_i", NP, I32)
        lo_h = sb("lo_h", NP, F16)
        lo_hot = attn_w[:, :].bitcast(F16)[:, 0:NP * P]
        cnt_i = sb("cnt_i", E, I32)
        tiles_i = sb("tiles_i", E, I32)
        tiles_of = sb("tiles_of", E)
        tiles_before = sb("tiles_before", E * E)
        first_slot = sb("first_slot", E)
        end_tile = sb("end_tile", E)
        hi_h = sb("hi_h", NP, F16)
        gate_hi = sb("gate_hi", NP, F16)
        gate_lo = sb("gate_lo", NP, F16)
        gate_rest = sb("gate_rest", NP)
        iota_h = sb("iota_h", P, F16)
        past = sb("past", SLOT_TILES * E)
        expert_f = sb("expert_f", SLOT_TILES)
        expert_off = sb("expert_off", SLOT_TILES, I32)
        load_need = sb("load_need", SLOT_TILES, I32)
        tiles_used = sb("tiles_used", 1, I32)
        warm_in = sb("warm_in", 512, BF16)
        HV = 3 * SLOT_TILES
        hi_hot = sb("hi_hot", NP * SLOT_TILES, F16)
        hi_val = wmod[:, :].bitcast(F16)[:, 0:NP * HV]
        slot_tab = sb("slot_tab", HV)
        slot_gate = sb("slot_gate", SLOT_TILES)
        empty = sb("empty", SLOT_TILES)
        row_from = sb("row_from", SLOT_TILES, U32)
        row_to = sb("row_to", SLOT_TILES, U32)
        from_now = sb("from_now", ROWS, U32)
        to_now = sb("to_now", 1, U32)
        rows = [work[:, 2 * n * D:2 * (n + 1) * D] for n in range(ROWS)]
        assert ROWS * 2 * D <= 2 * PB * D
        rest = work[:, 2 * ROWS * D:]
        rowsT = rest[:, 0:KD * P]
        y_gated = [stateT[:, 0:D], stateT[:, D:2 * D]]
        silu = rest[:, 2 * D:2 * D + I]
        act_ = rest[:, 2 * D + I:2 * D + 2 * I]
        actT = rest[:, 2 * D + 2 * I:2 * D + 2 * I + KI * P]

        ident = const[:, C_ID:C_ID + P]

        bank = [ctx.enter_context(nc.psum_tensor(f"bank{n}", [P, 512], F32)) for n in range(8)]
        xhatT_ps = bank[0:2]
        state_ps = bank[2]
        attn_ps = bank[3:5]
        c_ga_ps = bank[0:2]
        row_a_ps = bank[5:7]
        row_b_ps = bank[5:7]
        h2T_ps = bank[5:7]
        logit_ps = bank[7][:, 0:R]
        rank_ps = bank[2][:, 0:TE]
        count_ps = bank[7][:, 0:E]
        col_a_ps = bank[7]
        col_b_ps = bank[7]
        warm_ps = bank[0]
        tab_ps = bank[3]
        up1_ps, up3_ps = bank[0], bank[1]
        rowsT_ps = bank[2]
        actT_ps = bank[5]
        y_ps = bank[4]

        const_loaded = sem("const_loaded")
        cond_loaded = sem("cond_loaded")
        x_first_loaded = sem("x_batch0_loaded")
        x_second_loaded = sem("x_batch1_loaded")
        x_rest_loaded = sem("x_rest_loaded")
        small_loaded = sem("small_weights_loaded")
        wmod_a_loaded = sem("wmod_a_loaded")
        wmod_b_loaded = sem("wmod_b_loaded")
        warm_set = sem("warm_up_operand_set")
        w_loaded = sem("expert_weights_loaded")
        consts_set = sem("pool_constants_set")
        mod_stored = sem("mod_rows_stored")
        mod_spread = sem("mod_rows_spread")
        cond_done = sem("silu_of_cond_done")
        row_a_ready = sem("mod_rows_a_psum_ready")
        row_b_ready = sem("mod_rows_b_psum_ready")
        row_a_done = sem("mod_rows_a_copied")
        row_b_done = sem("mod_rows_b_copied")
        modrow_done = sem("mod_rows_done")
        col_a_ready = sem("mod_cols_a_psum_ready")
        col_b_ready = sem("mod_cols_b_psum_ready")
        modcol_done = sem("mod_cols_done")
        ga_d_ready = sem("ga_times_D_ready")
        c_scaled_ready = sem("c_scaled_ready")
        c_ga_ps_ready = sem("c_ga_psum_ready")
        c_ga_ready = sem("c_ga_ready")
        diag_ready = sem("diag_ready")
        var_ready = sem("var_eps_ready")
        rstd_ready = sem("rstd_ready")
        var2_ready = sem("var_eps2_ready")
        rstd2_ready = sem("rstd2_ready")
        shift2_ready = sem("shift2_ready")
        xhat_ready = sem("xhat_ready")
        xhatT_ready = sem("xhatT_psum_ready")
        hT_ready = sem("hT_ready")
        state_ps_ready = sem("state_psum_ready")
        state_ready = sem("state_ready")
        attn_ready = sem("attn_psum_ready")
        x1_ready = sem("x1_ready")
        xhat2_ready = sem("xhat2_ready")
        h2_scaled = sem("h2_scaled")
        h2_ready = sem("h2_ready")
        h2T_ps_ready = sem("h2T_psum_ready")
        h2T_ready = sem("h2T_ready")
        logits_ready = sem("logits_psum_ready")
        logits_out = sem("logits_copied")
        h2_stored = [sem("h2_rows_stored_even"), sem("h2_rows_stored_odd")]
        gb_stored = sem("gb_rows_stored")
        x1_stored = sem("x1_stored_to_output")
        both_ready = sem("both_choices_ready")
        dve_done = sem("vector_step_done")
        below_ready = sem("distances_ready")
        expo_ready = sem("exponentials_ready")
        keep_ready = sem("keep_masks_ready")
        sum_step = sem("sums_of_exponentials_step")
        gate_ready = sem("gates_ready")
        gate_hi_ready = sem("gates_high_part_ready")
        gate_rest_ready = sem("gates_rest_ready")
        gate_lo_ready = sem("gates_low_part_ready")
        rank_ready = sem("ranks_psum_ready")
        count_ready = sem("expert_totals_ready")
        lo_hot_ready = sem("slot_in_tile_one_hots_ready")
        tok_vals_ready = sem("token_values_ready")
        last_tok_ready = sem("last_token_values_ready")
        table_ps_ready = sem("slot_table_psum_ready")
        from_ready = sem("rows_to_fetch_ready")
        table_ready = sem("slot_tables_ready")
        hots_ready = sem("slot_tile_one_hots_ready")
        gate_vals_ready = sem("gate_values_ready")
        idx_ready = sem("row_indices_copied")
        rows_loaded = [sem(f"rows_gathered{n}") for n in range(ROWS)]
        rowsT_ps_ready = sem("rowsT_psum_ready")
        rowsT_ready = sem("rowsT_ready")
        up1_ready = sem("up1_psum_ready")
        up3_ready = sem("up3_psum_ready")
        silu_ready = sem("silu_ready")
        act_ready = sem("act_ready")
        actT_ps_ready = sem("actT_psum_ready")
        actT_ready = sem("actT_ready")
        y_ready = sem("y_psum_ready")
        y_gated_ready = sem("y_gated_ready")
        y_added = sem("y_added_to_output")

        block = ctx.enter_context(nc.Block())

        UNROLL = 4
        LAST = ALWAYS - 1
        HEAD = 2 + (LAST - 2) % UNROLL
        assert UNROLL == ROWS and (LAST - HEAD) % UNROLL == 0
        MORE = range(ALWAYS, SLOT_TILES)

        def slots_used(engine):
            return engine.value_load(tiles_used[0:1, 0:1], min_val=0, max_val=SLOT_TILES)

        @block.sync
        def _(sp):
            def x_rows(ap, b, n):
                return ap[b * SEQ:(b + n) * SEQ, :].rearrange("(j p) d -> p j d", p=P)

            def tiles(t, b, n):
                return t[:, b * PB * D:(b + n) * PB * D].rearrange("p (j d) -> p j d", d=D)

            def load_piece(n):
                part = WSTEP // PIECES
                sp.dma_start(w[:, bass.ds(n * part, part)], w_in[:, bass.ds(n * part, part)]).then_inc(w_loaded, 16)

            half = KD * MROW
            sp.dma_start(cond[:, :], cond_in).then_inc(cond_loaded, 16)
            sp.dma_start(tiles(x, 0, 1), x_rows(x_in, 0, 1)).then_inc(x_first_loaded, 16)
            sp.dma_start(wmod[:, 0:half], wmod_in[:, 0:half]).then_inc(wmod_a_loaded, 16)
            sp.dma_start(const[:, :], const_in).then_inc(const_loaded, 16)
            sp.dma_start(c_nat[:, :], c_in).then_inc(small_loaded, 16)
            sp.dma_start(bT[:, :], bT_in).then_inc(small_loaded, 16)
            sp.dma_start(dT[:, :], dT_in).then_inc(small_loaded, 16)
            sp.dma_start(gw[:, :], gw_in).then_inc(small_loaded, 16)
            sp.dma_start(wmod[:, half:2 * half], wmod_in[:, half:2 * half]).then_inc(wmod_b_loaded, 16)
            sp.dma_start(tiles(x, 1, 1), x_rows(x_in, 1, 1)).then_inc(x_second_loaded, 16)
            sp.dma_start(tiles(x, 2, 2), x_rows(x_in, 2, 2)).then_inc(x_rest_loaded, 16)
            sp.wait_ge(modrow_done, 1)
            sp.dma_start(mod_dram, mod_row[0:BATCH, MROW:2 * MROW]).then_inc(mod_stored, 16)
            sp.wait_ge(mod_stored, 16)
            sp.dma_start(mod_all[:, :], mod_dram.rearrange("(a b) c -> a (b c)", a=1).to_broadcast((P, BATCH * MROW)))\
                .then_inc(mod_spread, 16)
            sp.wait_ge(mod_spread, 16)
            with sp.Fori(0, BATCH) as b:
                sp.dma_start(h2_dram[bass.ds(b * SEQ, SEQ), D:2 * D].rearrange("(j p) d -> p j d", p=P),
                             mod_all[:, bass.ds(b * MROW + 2 * D, D)].unsqueeze(1).to_broadcast((P, PB, D)))\
                    .then_inc(gb_stored, 16)
            for n in range(PIECES):
                load_piece(n)
            with sp.Fori(0, BATCH // 2) as pair:
                for odd in range(2):
                    b = pair * 2 + odd
                    sp.wait_ge(x1_ready, 2 * b + 2)
                    sp.dma_start(out[bass.ds(b * SEQ, SEQ), :].rearrange("(j p) d -> p j d", p=P),
                                 x[:, bass.ds(b * (PB * D), PB * D)].rearrange("p (j d) -> p j d", d=D))\
                        .then_inc(x1_stored, 16)
                    sp.wait_ge(h2_ready, b + 1)
                    sp.dma_start(h2_dram[bass.ds(b * SEQ, SEQ), 0:D].rearrange("(j p) d -> p j d", p=P),
                                 h2[:, odd * PB * D:(odd + 1) * PB * D].rearrange("p (j d) -> p j d", d=D))\
                        .then_inc(h2_stored[odd], 16)
            with sp.Fori(PIECES, PIECES * E) as n:
                sp.wait_ge(w_loaded, 16 * n)
                load_piece(n)

        NG = NP // GROUPS
        SUM_STEPS = 4
        assert E == 1 << (SUM_STEPS - 1)
        CHOICE_PARTS = ((0, TILES - PB), (TILES - PB, TILES))

        def by_tile(ap, g):
            return ap[:, g * NG:(g + 1) * NG].unsqueeze(2).to_broadcast((P, NG, SLOT_TILES))

        def tile_hots(g):
            return hi_hot[:, g * NG * SLOT_TILES:(g + 1) * NG * SLOT_TILES].rearrange("p (n s) -> p n s", s=SLOT_TILES)

        def tile_values(g, m):
            vals = hi_val[:, g * NG * HV:(g + 1) * NG * HV].rearrange("p (n v) -> p n v", v=HV)
            return vals[:, :, m * SLOT_TILES:(m + 1) * SLOT_TILES]

        @block.gpsimd
        def _(pool):
            pool.memset(warm_in[:, :], 1.0).then_inc(warm_set, 1)
            pool.memset(minus_half[:, :], -0.5).then_inc(consts_set, 1)
            pool.memset(ones_b[:, :], 1.0).then_inc(consts_set, 1)
            pool.wait_ge(consts_set, 2)

            def power1(b):
                pool.wait_ge(var_ready, b + 1)
                pool.tensor_tensor(rstd[:, :], var_eps[:, :], minus_half[:, :], ALU.pow).then_inc(rstd_ready, 1)

            def power2(b):
                pool.wait_ge(var2_ready, b + 1)
                if b:
                    pool.wait_ge(xhat2_ready, PB * b)
                pool.tensor_tensor(rstd2[:, :], var_eps2[:, :], minus_half[:, :], ALU.pow).then_inc(rstd2_ready, 1)
                pool.wait_ge(rstd2_ready, b + 1)
                pool.tensor_tensor(shift2[:, :], minus_mean2[:, :], rstd2[:, :], ALU.mult).then_inc(shift2_ready, 1)

            def row(b, m):
                return mod_all[:, b * MROW + m * D:b * MROW + (m + 1) * D].unsqueeze(1).to_broadcast((P, PB, D))

            def h2_tiles(b):
                return h2[:, (b % 2) * PB * D:(b % 2 + 1) * PB * D].rearrange("p (j d) -> p j d", d=D)

            def scale_h2(b):
                pool.wait_ge(xhat2_ready, PB * (b + 1))
                if b >= 2:
                    pool.wait_ge(h2_stored[b % 2], 16 * (b // 2))
                pool.tensor_tensor(h2_tiles(b), xhat2[b % 2].rearrange("p (j d) -> p j d", d=D), row(b, 1), ALU.mult)\
                    .then_inc(h2_scaled, 1)

            def shift_h2(b):
                pool.wait_ge(h2_scaled, b + 1)
                pool.tensor_tensor(h2_tiles(b), h2_tiles(b), row(b, 0), ALU.add).then_inc(h2_ready, 1)

            power1(0)
            power1(1)
            power1(2)
            power2(0)
            power1(3)
            pool.wait_ge(mod_spread, 16)
            scale_h2(0)
            power2(1)
            shift_h2(0)
            scale_h2(1)
            power2(2)
            shift_h2(1)
            power2(3)
            for b in (2, 3):
                scale_h2(b)
                shift_h2(b)

            pool.wait_ge(expo_ready, 2 * TOPK)
            pool.wait_ge(keep_ready, 2 * TOPK)
            pool.tensor_tensor(keep[:, :], keep[:, :], expo[:, :], ALU.mult).then_inc(sum_step, 1)
            kept = keep[:, :].rearrange("p (n e) -> p n e", e=E)
            for step in range(1, SUM_STEPS):
                n = E >> step
                pool.wait_ge(sum_step, step)
                pool.tensor_tensor(kept[:, :, 0:n] if n > 1 else expo_sum[:, :].unsqueeze(2),
                                   kept[:, :, 0:n], kept[:, :, n:2 * n], ALU.add).then_inc(sum_step, 1)
            pool.wait_ge(gate_hi_ready, 1)
            pool.tensor_tensor(gate_rest[:, :], gate[:, :], gate_hi[:, :], ALU.subtract).then_inc(gate_rest_ready, 1)
            pool.wait_ge(gate_lo_ready, 1)
            for g in range(GROUPS):
                pool.wait_ge(hots_ready, g + 1)
                for m, val in enumerate((gate_hi, gate_lo)):
                    pool.tensor_tensor(tile_values(g, m + 1), tile_hots(g), by_tile(val, g), ALU.mult)\
                        .then_inc(gate_vals_ready, 1)

            copies = pool.alloc_register("index_copies")

            def copy_index(now, table, s, count):
                pool.tensor_copy(now, table[:, bass.ds(s, 1)]).then_inc(idx_ready, 1)
                if count is None:
                    pool.reg_add(copies, copies, 1)
                    count = copies
                pool.wait_ge(gb_stored, 16 * BATCH)
                pool.wait_ge(idx_ready, count)

            def fetch(s, h, count=None):
                copy_index(from_now[:, h:h + 1], row_from, s, count)
                pool.indirect_dma_start(rows[h], None, h2_dram,
                                        bass.IndirectOffsetOnAxis(ap=from_now[:, h:h + 1], axis=0))\
                    .then_inc(rows_loaded[h], 16)

            def add_back(s, h, count=None):
                pool.wait_ge(y_gated_ready, s + 1)
                copy_index(to_now[:, :], row_to, s, count)
                pool.indirect_dma_start(out, bass.IndirectOffsetOnAxis(ap=to_now[:, :], axis=0), y_gated[h % 2],
                                        None, compute_op=ALU.add).then_inc(y_added, 16)

            pool.wait_ge(from_ready, 1)
            for odd in range(2):
                pool.wait_ge(h2_stored[odd], 16 * BATCH // 2)
            pool.wait_ge(x1_stored, 16 * BATCH)
            fetch(0, 0, 1)
            fetch(1, 1, 2)
            fetch(2, 2, 3)
            pool.wait_ge(table_ready, 1)
            done = 3
            for s in range(1, HEAD):
                fetch(s + 2, (s + 2) % ROWS, done + 1)
                if s >= 2:
                    pool.wait_ge(y_added, 16 * (s - 1))
                add_back(s - 1, (s - 1) % ROWS, done + 2)
                done += 2
            pool.reg_mov(copies, done)
            with pool.Fori(0, (LAST - HEAD) // UNROLL - 1) as r:
                s0 = r * UNROLL + HEAD
                for u in range(UNROLL):
                    fetch(s0 + u + 2, (HEAD + u + 2) % ROWS)
                    pool.wait_ge(y_added, 16 * (s0 + u - 1))
                    add_back(s0 + u - 1, (HEAD + u - 1) % ROWS)
            s0 = LAST - UNROLL
            done += 2 * (s0 - HEAD)

            used = slots_used(pool)
            for s in range(s0, LAST + 2):
                if s + 2 <= LAST:
                    fetch(s + 2, (s + 2) % ROWS, done + 1)
                    done += 1
                pool.wait_ge(y_added, 16 * (s - 1))
                add_back(s - 1, (s - 1) % ROWS, done + 1)
                done += 1
            with pool.If(used > ALWAYS):
                for s in MORE:
                    fetch(s, s % ROWS, done + 1)
                    done += 1
                for s in MORE:
                    pool.wait_ge(y_added, 16 * s)
                    add_back(s, s % ROWS, done + 1)
                    done += 1
                pool.wait_ge(y_added, 16 * SLOT_TILES)
            pool.wait_ge(y_added, 16 * ALWAYS)

        @block.scalar
        def _(act):
            act.wait_ge(cond_loaded, 16)
            act.activation(cond_silu[:, :], cond[:, :], ACT.Silu).then_inc(cond_done, 1)

            def modulate(b):
                for k in range(KD):
                    act.wait_ge(xhatT_ready, KD * b + k + 1)
                    act.activation(hT[:, k * SEQ:(k + 1) * SEQ], xhatT_ps[k][:, :], ACT.Identity,
                                   bias=mod_col[:, k * BATCH + b:k * BATCH + b + 1],
                                   scale=mod_col[:, WC + k * BATCH + b:WC + k * BATCH + b + 1]).then_inc(hT_ready, 1)

            def state(b):
                act.wait_ge(state_ps_ready, b + 1)
                act.activation(stateT[:, :], state_ps[:, :], ACT.Tanh).then_inc(state_ready, 1)

            def normalize2(b):
                act.wait_ge(shift2_ready, b + 1)
                if b >= 2:
                    act.wait_ge(h2_scaled, b - 1)
                    act.wait_ge(h2T_ps_ready, b - 1)
                for q in range(PB):
                    act.activation(xhat2[b % 2][:, q * D:(q + 1) * D], x[:, (b * PB + q) * D:(b * PB + q + 1) * D], ACT.Identity,
                                   bias=shift2[:, q:q + 1], scale=rstd2[:, q:q + 1]).then_inc(xhat2_ready, 1)

            def modulate2(b):
                for k in range(KD):
                    act.wait_ge(h2T_ps_ready, b + 1)
                    act.activation(h2T[:, k * SEQ:(k + 1) * SEQ], h2T_ps[k][:, :], ACT.Identity,
                                   bias=mod_col[:, 3 * WC + k * BATCH + b:3 * WC + k * BATCH + b + 1],
                                   scale=mod_col[:, 4 * WC + k * BATCH + b:4 * WC + k * BATCH + b + 1]).then_inc(h2T_ready, 1)

            act.wait_ge(row_a_ready, 1)
            act.activation(mod_row[0:BATCH, 2 * D:3 * D], row_a_ps[1][0:BATCH, 0:D], ACT.Copy).then_inc(row_a_done, 1)
            act.wait_ge(modcol_done, 1)
            modulate(0)

            def diagonals(b):
                for k in range(KD):
                    last = act.activation(diag[:, b * D + k * P:b * D + (k + 1) * P], ident, ACT.Copy,
                                          scale=ga_d[:, k * BATCH + b:k * BATCH + b + 1])
                last.then_inc(diag_ready, 1)

            def copy_c_ga(n):
                act.wait_ge(c_ga_ps_ready, n + 1)
                act.activation(c_ga[:, n * 512:(n + 1) * 512], c_ga_ps[n][:, :], ACT.Copy).then_inc(c_ga_ready, 1)

            act.wait_ge(const_loaded, 16)
            act.wait_ge(ga_d_ready, 1)
            diagonals(0)
            copy_c_ga(0)
            state(0)
            copy_c_ga(1)
            for b in range(1, BATCH):
                diagonals(b)
            for b in range(BATCH):
                if b + 1 < BATCH:
                    act.wait_ge(attn_ready, 2 * (b + 1))
                    modulate(b + 1)
                    state(b + 1)
                if b == 1:
                    act.wait_ge(modcol_done, 2)
                if b >= 2:
                    act.wait_ge(logits_ready, b - 1)
                if b >= 1:
                    modulate2(b - 1)
                normalize2(b)
            act.wait_ge(logits_ready, BATCH - 1)
            modulate2(BATCH - 1)
            for n, (j0, j1) in enumerate(CHOICE_PARTS):
                for c in range(TOPK):
                    cols = slice(c * TE + j0 * E, c * TE + j1 * E)
                    act.wait_ge(below_ready, TOPK * n + c + 1)
                    act.activation(expo[:, cols], below[:, cols], ACT.Exp, scale=-1.0).then_inc(expo_ready, 1)
            act.wait_ge(gate_ready, 1)
            act.activation(gate_hi[:, :], gate[:, :], ACT.Copy).then_inc(gate_hi_ready, 1)
            act.wait_ge(gate_rest_ready, 1)
            act.activation(gate_lo[:, :], gate_rest[:, :], ACT.Copy, scale=2048.0).then_inc(gate_lo_ready, 1)
            for g in range(GROUPS - 1):
                act.wait_ge(hots_ready, g + 1)
                for n in range(NG):
                    act.activation(tile_values(g, 0)[:, n, :], tile_hots(g)[:, n, :], ACT.Copy,
                                   scale=const[:, C_TOK + g * NG + n:C_TOK + g * NG + n + 1]).then_inc(tok_vals_ready, 1)
            act.activation(cond_silu[:, :], cond[:, :], ACT.Silu)

            def copy_rowsT(s):
                act.wait_ge(rowsT_ps_ready, s + 1)
                act.activation(rowsT, rowsT_ps[:, 0:KD * P], ACT.Copy).then_inc(rowsT_ready, 1)

            act.wait_ge(table_ready, 1)
            used = slots_used(act)
            copy_rowsT(0)

            def tile(s, more=True):
                act.wait_ge(up1_ready, s + 1)
                act.activation(silu, up1_ps[:, :], ACT.Silu).then_inc(silu_ready, 1)
                if more:
                    copy_rowsT(s + 1)
                act.wait_ge(actT_ps_ready, s + 1)
                act.activation(actT, actT_ps[:, :], ACT.Copy).then_inc(actT_ready, 1)

            for s in range(HEAD):
                tile(s)
            with act.Fori(0, (LAST - HEAD) // UNROLL) as r:
                s0 = r * UNROLL + HEAD
                for u in range(UNROLL):
                    tile(s0 + u)
            tile(LAST, False)
            with act.If(used > ALWAYS):
                copy_rowsT(ALWAYS)
                for s in MORE:
                    tile(s, s + 1 < SLOT_TILES)

        @block.tensor
        def _(pe):
            def transpose_xhat(b):
                pe.wait_ge(xhat_ready, b + 1)
                for k in range(KD):
                    for q in range(PB):
                        last = pe.transpose(xhatT_ps[k][:, q * P:(q + 1) * P],
                                            xhat[:, q * D + k * P:q * D + (k + 1) * P], ident)
                    last.then_inc(xhatT_ready, 1)

            def mod_rows(ps, half):
                for n, (col, width) in enumerate(((0, 512), (512, 256))):
                    for k in range(KD):
                        c0 = (half * KD + k) * MROW + col
                        last = pe.matmul(ps[n][0:BATCH, 0:width], cond_silu[:, k * BATCH:(k + 1) * BATCH],
                                         wmod[:, c0:c0 + width], start=(k == 0), stop=(k == KD - 1))
                return last

            def mod_columns(ps, ms):
                for n, m in enumerate(ms):
                    for c in range(KD):
                        last = pe.matmul(ps[:, n * WC + c * BATCH:n * WC + (c + 1) * BATCH],
                                         mod_row[0:BATCH, m * D + c * P:m * D + (c + 1) * P], ident[0:BATCH, 0:BATCH],
                                         start=True, stop=True)
                return last

            def keep_warm(n):
                for _ in range(n):
                    pe.matmul(warm_ps[:, :], warm_in[:, 0:P], warm_in[:, :], start=True, stop=True)

            def state_in(b):
                for k in range(KD):
                    pe.wait_ge(hT_ready, KD * b + k + 1)
                    last = pe.matmul(state_ps[:, :], bT[:, k * NSTATE:(k + 1) * NSTATE], hT[:, k * SEQ:(k + 1) * SEQ],
                                     start=(k == 0), stop=(k == KD - 1))
                last.then_inc(state_ps_ready, 1)

            def attn(b):
                pe.wait_ge(diag_ready, b + 1)
                pe.wait_ge(c_ga_ready, b // 2 + 1)
                pe.wait_ge(state_ready, b + 1)
                for q in range(PB):
                    o = attn_ps[q // 2]
                    c0 = (q % 2) * D
                    pe.matmul(o[:, c0:c0 + D], stateT[:, q * P:(q + 1) * P], c_ga[:, b * D:(b + 1) * D],
                              start=True, stop=False)
                    for k in range(KD):
                        last = pe.matmul(o[:, c0 + k * P:c0 + (k + 1) * P], hT[:, k * SEQ + q * P:k * SEQ + (q + 1) * P],
                                         diag[:, b * D + k * P:b * D + (k + 1) * P], start=False, stop=(k == KD - 1))
                    if q % 2:
                        last.then_inc(attn_ready, 1)

            def transpose_xhat2(b):
                for q in range(PB):
                    pe.wait_ge(xhat2_ready, PB * b + q + 1)
                    for k in range(KD):
                        last = pe.transpose(h2T_ps[k][:, q * P:(q + 1) * P],
                                            xhat2[b % 2][:, q * D + k * P:q * D + (k + 1) * P], ident)
                last.then_inc(h2T_ps_ready, 1)

            def logits(b):
                pe.wait_ge(h2T_ready, KD * (b + 1))
                for q in range(PB):
                    for k in range(KD):
                        last = pe.matmul(logit_ps[:, q * E:(q + 1) * E],
                                         h2T[:, k * SEQ + q * P:k * SEQ + (q + 1) * P], gw[:, k * E:(k + 1) * E],
                                         start=(k == 0), stop=(k == KD - 1))
                last.then_inc(logits_ready, 1)

            pe.wait_ge(warm_set, 1)
            keep_warm(14)
            pe.wait_ge(cond_done, 1)
            pe.wait_ge(wmod_a_loaded, 16)
            mod_rows(row_a_ps, 0).then_inc(row_a_ready, 1)
            pe.wait_ge(const_loaded, 16)
            transpose_xhat(0)
            pe.wait_ge(row_a_done, 2)
            mod_columns(col_a_ps, (0, 1, 2)).then_inc(col_a_ready, 1)
            pe.wait_ge(wmod_b_loaded, 16)
            mod_rows(row_b_ps, 1).then_inc(row_b_ready, 1)

            def transpose_c(n):
                pe.wait_ge(hT_ready, n + 1)
                pe.wait_ge(c_scaled_ready, n + 1)
                for i in range(4):
                    last = pe.transpose(c_ga_ps[n][:, i * P:(i + 1) * P], c_scaled[:, (4 * n + i) * P:(4 * n + i + 1) * P],
                                        ident)
                last.then_inc(c_ga_ps_ready, 1)

            transpose_c(0)
            pe.wait_ge(small_loaded, 64)
            state_in(0)
            transpose_c(1)
            for b in range(BATCH):
                if b >= 1:
                    pe.wait_ge(x1_ready, 2 * b)
                attn(b)
                if b == 0:
                    pe.wait_ge(c_ga_ready, 2)
                if b + 1 < BATCH:
                    transpose_xhat(b + 1)
                if b == 0:
                    pe.wait_ge(row_b_done, 2)
                    pe.wait_ge(modcol_done, 1)
                    mod_columns(col_b_ps, (3, 4)).then_inc(col_b_ready, 1)
                if b >= 2:
                    pe.wait_ge(h2T_ready, KD * (b - 1))
                if b >= 1:
                    transpose_xhat2(b - 1)
                if b + 1 < BATCH:
                    state_in(b + 1)
                if b == 2:
                    pe.wait_ge(modcol_done, 2)
                if b >= 3:
                    pe.wait_ge(logits_out, b - 2)
                if b >= 2:
                    logits(b - 2)
            keep_warm(6)
            pe.wait_ge(logits_out, BATCH - 2)
            logits(BATCH - 2)
            transpose_xhat2(BATCH - 1)
            keep_warm(5)
            pe.wait_ge(logits_out, BATCH - 1)
            logits(BATCH - 1)
            keep_warm(10)

            pe.wait_ge(both_ready, 2)
            for j in range(TILES):
                last = pe.matmul(count_ps, ones_b[:, :], both[:, j * E:(j + 1) * E],
                                 start=(j == 0), stop=(j == TILES - 1))
            last.then_inc(count_ready, 1)
            pe.matmul(rank_ps, upper_b[:, :], both[:, :], start=True, stop=False)
            for d in range(1, TILES):
                last = pe.matmul(rank_ps[:, d * E:TE], ones_b[:, :], both[:, 0:TE - d * E],
                                 start=False, stop=(d == TILES - 1))
            last.then_inc(rank_ready, 1)
            keep_warm(28)
            for g in range(GROUPS):
                pe.wait_ge(lo_hot_ready, g + 1)
                if g < GROUPS - 1:
                    pe.wait_ge(tok_vals_ready, NG * (g + 1))
                else:
                    pe.wait_ge(last_tok_ready, 1)
                pe.wait_ge(gate_vals_ready, 2 * (g + 1))
                for n in range(g * NG, (g + 1) * NG):
                    last = pe.matmul(tab_ps[:, 0:HV], lo_hot[:, n * P:(n + 1) * P], hi_val[:, n * HV:(n + 1) * HV],
                                     start=(n == 0), stop=(n == NP - 1))
            last.then_inc(table_ps_ready, 1)

            keep_warm(19)

            def transpose_rows(s, h, count):
                pe.wait_ge(rows_loaded[h], count)
                for k in range(KD):
                    last = pe.transpose(rowsT_ps[:, k * P:(k + 1) * P], rows[h][:, k * P:(k + 1) * P], ident)
                last.then_inc(rowsT_ps_ready, 1)

            def weights_needed(s):
                return pe.value_load(load_need[0:1, bass.ds(s, 1)], min_val=16 * PIECES, max_val=16 * PIECES * E)

            def up(s, off, need):
                pe.wait_ge(rowsT_ready, s + 1)
                pe.wait_ge(w_loaded, need)
                for m, ps, done in ((0, up1_ps, up1_ready), (W3, up3_ps, up3_ready)):
                    for k in range(KD):
                        last = pe.matmul(ps[:, :], rowsT[:, k * P:(k + 1) * P], w[:, bass.ds(off + m + k * I, I)],
                                         start=(k == 0), stop=(k == KD - 1))
                    last.then_inc(done, 1)

            def down(s, off):
                pe.wait_ge(actT_ready, s + 1)
                for k in range(KI):
                    last = pe.matmul(y_ps[:, 0:D], actT[:, k * P:(k + 1) * P], w[:, bass.ds(off + W2 + k * D, D)],
                                     start=(k == 0), stop=(k == KI - 1))
                last.then_inc(y_ready, 1)

            def transpose_act(s):
                pe.wait_ge(act_ready, s + 1)
                for k in range(KI):
                    last = pe.transpose(actT_ps[:, k * P:(k + 1) * P], act_[:, k * P:(k + 1) * P], ident)
                last.then_inc(actT_ps_ready, 1)

            def weight_column(s):
                return pe.value_load(expert_off[0:1, bass.ds(s, 1)], min_val=0, max_val=(E - 1) * WSTEP)

            pe.wait_ge(table_ready, 1)
            first_off, first_need = weight_column(0), weights_needed(0)
            transpose_rows(0, 0, 16)
            up(0, first_off, first_need)

            def step(s, h, count, off, with_down=True):
                off = off + [weight_column(s + 1)]
                need = weights_needed(s + 1)
                transpose_rows(s + 1, h, count)
                if with_down:
                    down(s - 1, off[0])
                transpose_act(s)
                up(s + 1, off[2], need)
                return off[1:]

            off = [None, first_off]
            off = step(0, 1, 16, off, False)
            for s in range(1, HEAD):
                if s >= 2:
                    pe.wait_ge(y_gated_ready, s - 1)
                off = step(s, (s + 1) % ROWS, 16 * ((s + 1) // ROWS + 1), off)
            with pe.Fori(0, (LAST - HEAD) // UNROLL) as r:
                s0 = r * UNROLL + HEAD
                off = [weight_column(s0 - 1), weight_column(s0)]
                for u in range(UNROLL):
                    s = s0 + u
                    pe.wait_ge(y_gated_ready, s - 1)
                    off = step(s, (HEAD + u + 1) % ROWS, 16 * (r + (HEAD + u + 1) // ROWS + 1), off)

            def finish(last):
                pe.wait_ge(y_gated_ready, last - 1)
                down(last - 1, weight_column(last - 1))
                transpose_act(last)
                pe.wait_ge(y_gated_ready, last)
                down(last, weight_column(last))

            used = slots_used(pe)
            finish(LAST)
            with pe.If(used > ALWAYS):
                transpose_rows(ALWAYS, ALWAYS % ROWS, 16 * (ALWAYS // ROWS + 1))
                up(ALWAYS, weight_column(ALWAYS), weights_needed(ALWAYS))
                off = [None, weight_column(ALWAYS)]
                for s in MORE[:-1]:
                    pe.wait_ge(y_gated_ready, s - 1)
                    off = step(s, (s + 1) % ROWS, 16 * ((s + 1) // ROWS + 1), off, s > ALWAYS)
                finish(SLOT_TILES - 1)

        @block.vector
        def _(dve):
            steps = [0]

            def link(ins):
                ins.then_inc(dve_done, 1)
                steps[0] += 1
                dve.wait_ge(dve_done, steps[0])

            def x_tile(b, q):
                return x[:, (b * PB + q) * D:(b * PB + q + 1) * D]

            def moments(st, mv):
                for q in range(PB):
                    last = dve.bn_aggr(mv[:, q * 2:(q + 1) * 2], st[:, q * 6:(q + 1) * 6])
                link(last)

            def statistics(b):
                for q in range(PB):
                    last = dve.bn_stats(stats[:, q * 6:(q + 1) * 6], x_tile(b, q))
                link(last)
                moments(stats, mean_var)
                dve.tensor_scalar(var_eps[:, :], mean_var[:, 1:2 * PB:2], EPS, None, ALU.add).then_inc(var_ready, 1)

            def normalize(b):
                dve.wait_ge(rstd_ready, b + 1)
                if b:
                    dve.wait_ge(xhatT_ready, KD * b)
                for q in range(PB):
                    last = dve.tensor_scalar(xhat[:, q * D:(q + 1) * D], x_tile(b, q),
                                             mean_var[:, 2 * q:2 * q + 1], rstd[:, q:q + 1],
                                             ALU.subtract, ALU.mult)
                last.then_inc(xhat_ready, 1)

            def residual(b):
                for g in range(2):
                    dve.wait_ge(attn_ready, 2 * b + g + 1)
                    xs = x[:, (b * PB + 2 * g) * D:(b * PB + 2 * g + 2) * D]
                    dve.tensor_tensor(xs, attn_ps[g][:, :], xs, ALU.add).then_inc(x1_ready, 1)
                    dve.wait_ge(x1_ready, 2 * b + g + 1)
                    for q in (2 * g, 2 * g + 1):
                        last = dve.bn_stats(stats2[:, q * 6:(q + 1) * 6], x_tile(b, q))
                link(last)
                moments(stats2, mean_var2)
                if b:
                    dve.wait_ge(shift2_ready, b)
                dve.tensor_scalar(minus_mean2[:, :], mean_var2[:, 0:2 * PB:2], -1.0, None, ALU.mult)
                dve.tensor_scalar(var_eps2[:, :], mean_var2[:, 1:2 * PB:2], EPS, None, ALU.add).then_inc(var2_ready, 1)

            def copy_logits(b):
                dve.wait_ge(logits_ready, b + 1)
                dve.tensor_copy(logit[:, b * R:(b + 1) * R], logit_ps).then_inc(logits_out, 1)

            def clamp_gate(out_, in_, t_sign, t_abs):
                dve.tensor_scalar(t_sign, in_, 0.0, 2.0, ALU.is_ge, ALU.mult)
                link(dve.scalar_tensor_tensor(t_abs, in_, -1.0, in_, ALU.mult, ALU.max))
                link(dve.tensor_scalar(t_abs, t_abs, 0.25, None, ALU.max))
                return dve.scalar_tensor_tensor(out_, t_sign, -1.0, t_abs, ALU.add, ALU.mult)

            dve.wait_ge(x_first_loaded, 16)
            statistics(0)
            normalize(0)
            dve.wait_ge(row_a_ready, 1)
            dve.tensor_copy(mod_row[0:BATCH, 0:D], row_a_ps[0][0:BATCH, 0:D])
            dve.tensor_scalar(mod_row[0:BATCH, D:2 * D], row_a_ps[0][0:BATCH, D:2 * D], 1.0, None, ALU.add)\
                .then_inc(row_a_done, 1)
            dve.wait_ge(const_loaded, 16)
            dve.tensor_copy(upper_b[:, :], const[:, C_UP:C_UP + P])
            dve.tensor_copy(iota_h[:, :], const[:, C_IOTA:C_IOTA + P])

            dve.wait_ge(col_a_ready, 1)
            dve.tensor_copy(mod_col[:, 0:3 * WC], col_a_ps[:, 0:3 * WC]).then_inc(modcol_done, 1)
            dve.wait_ge(modcol_done, 1)
            ga = mod_col[:, 2 * WC:3 * WC]
            link(clamp_gate(ga, ga, gate_tmp[:, 0:WC], gate_tmp[:, WC:2 * WC]))
            dve.wait_ge(small_loaded, 64)
            dve.tensor_tensor(ga_d[:, :].rearrange("p (k b) -> p k b", b=BATCH),
                              ga.rearrange("p (k b) -> p k b", b=BATCH),
                              dT[:, :].unsqueeze(2).to_broadcast((P, KD, BATCH)), ALU.mult).then_inc(ga_d_ready, 1)
            for b in range(BATCH):
                for k in range(KD):
                    last = dve.tensor_scalar(c_scaled[:, (b * KD + k) * P:(b * KD + k + 1) * P],
                                             c_nat[:, k * P:(k + 1) * P],
                                             mod_col[:, 2 * WC + k * BATCH + b:2 * WC + k * BATCH + b + 1], None, ALU.mult)
                if b % 2:
                    last.then_inc(c_scaled_ready, 1)
            dve.wait_ge(x_second_loaded, 16)
            statistics(1)
            dve.wait_ge(row_b_ready, 1)
            g0, g1 = row_b_ps
            gb = mod_row[0:BATCH, MROW + 2 * D:2 * MROW]
            dve.tensor_copy(mod_row[0:BATCH, MROW:MROW + D], g0[0:BATCH, 0:D])
            dve.tensor_scalar(mod_row[0:BATCH, MROW + D:MROW + 2 * D], g0[0:BATCH, D:2 * D], 1.0, None, ALU.add)\
                .then_inc(row_b_done, 1)
            dve.tensor_copy(gb, g1[0:BATCH, 0:D]).then_inc(row_b_done, 1)
            normalize(1)
            dve.wait_ge(row_b_done, 2)
            clamp_gate(gb, gb, row_tmp[0:BATCH, 0:D], row_tmp[0:BATCH, D:2 * D]).then_inc(modrow_done, 1)
            dve.wait_ge(x_rest_loaded, 16)
            statistics(2)
            residual(0)
            dve.wait_ge(col_b_ready, 1)
            dve.tensor_copy(mod_col[:, 3 * WC:5 * WC], col_b_ps[:, 0:2 * WC]).then_inc(modcol_done, 1)
            for b in range(1, BATCH):
                if b + 1 < BATCH:
                    normalize(b + 1)
                if b + 2 < BATCH:
                    statistics(b + 2)
                residual(b)
                if b >= 2:
                    copy_logits(b - 2)

            def je(ap):
                return ap.rearrange("p (j e) -> p j e", e=E)

            def part(t, c, j0, j1, width=E):
                return t[:, (c * TILES + j0) * width:(c * TILES + j1) * width]

            def choose(j0, j1):
                n = j1 - j0
                tie_w = const[:, C_TIE:C_TIE + E].unsqueeze(1).to_broadcast((P, n, E))
                ties = je(part(tie, 0, j0, j1))
                tie_top = part(tie_max, 0, j0, j1, 1)
                link(dve.scalar_tensor_tensor(part(logit_abs, 0, j0, j1), part(logit, 0, j0, j1), -1.0,
                                              part(logit, 0, j0, j1), ALU.mult, ALU.max))
                for c in range(TOPK):
                    score, picks = je(part(logit, c, j0, j1)), je(part(pick, c, j0, j1))
                    tops = part(top, c, j0, j1, 1)
                    link(dve.tensor_reduce(tops, score, AX_X, ALU.max))
                    link(dve.tensor_tensor(picks, score, tops.unsqueeze(2).to_broadcast((P, n, E)), ALU.is_equal))
                    link(dve.tensor_tensor(ties, picks, tie_w, ALU.mult))
                    link(dve.tensor_reduce(tie_top, ties, AX_X, ALU.max))
                    link(dve.tensor_tensor(picks, ties, tie_top.unsqueeze(2).to_broadcast((P, n, E)), ALU.is_equal))
                    if c == 0:
                        link(dve.scalar_tensor_tensor(je(part(logit, 1, j0, j1)), picks, FAR, score, ALU.mult, ALU.add))
                dve.tensor_tensor(part(both, 0, j0, j1), part(pick, 0, j0, j1), part(pick, 1, j0, j1), ALU.add)\
                    .then_inc(both_ready, 1)

            def thresholds(j0, j1, n_before):
                n = j1 - j0
                for c in range(TOPK):
                    tops = part(top, c, j0, j1, 1).unsqueeze(2).to_broadcast((P, n, E))
                    far, scales = je(part(below, c, j0, j1)), je(part(scale, c, j0, j1))
                    dve.tensor_tensor(far, tops, je(part(logit, c, j0, j1)), ALU.subtract).then_inc(below_ready, 1)
                    link(dve.tensor_tensor(scales, je(part(logit_abs, 0, j0, j1)), tops, ALU.max))
                    dve.wait_ge(below_ready, n_before + c + 1)
                    dve.scalar_tensor_tensor(je(part(keep, c, j0, j1)), scales, JITTER2, far,
                                             ALU.mult, ALU.is_ge).then_inc(keep_ready, 1)

            copy_logits(BATCH - 2)
            dve.wait_ge(logits_out, BATCH - 1)
            choose(*CHOICE_PARTS[0])
            thresholds(*CHOICE_PARTS[0], 0)
            copy_logits(BATCH - 1)
            dve.wait_ge(logits_out, BATCH)
            choose(*CHOICE_PARTS[1])
            thresholds(*CHOICE_PARTS[1], TOPK)
            dve.wait_ge(count_ready, 1)
            link(dve.tensor_scalar(cnt_i[:, :], count_ps, float(P - 1), None, ALU.add))
            link(dve.tensor_scalar(tiles_i[:, :], cnt_i[:, :], 7, None, ALU.arith_shift_right))
            link(dve.tensor_copy(tiles_of[:, :], tiles_i[:, :]))
            link(dve.tensor_tensor(je(tiles_before[:, :]), tiles_of[:, :].unsqueeze(1).to_broadcast((P, E, E)),
                                   je(const[:, C_BEFORE:C_BEFORE + E * E]), ALU.mult))
            link(dve.tensor_reduce(first_slot[:, :], je(tiles_before[:, :]), AX_X, ALU.add))
            dve.wait_ge(rank_ready, 1)
            link(dve.tensor_tensor(je(slot_of[:, :]), je(rank_ps), first_slot[:, :].unsqueeze(1).to_broadcast((P, TILES, E)),
                                   ALU.add))
            link(dve.tensor_tensor(slot_pick[:, :].rearrange("p (c r) -> p c r", r=TE),
                                   pick[:, :].rearrange("p (c r) -> p c r", r=TE),
                                   slot_of[:, :].unsqueeze(1).to_broadcast((P, TOPK, TE)), ALU.mult))
            link(dve.tensor_reduce(slot[:, :], je(slot_pick[:, :]), AX_X, ALU.add))
            link(dve.tensor_copy(slot_i[:, :], slot[:, :]))
            dve.tensor_scalar(lo_i[:, :], slot_i[:, :], P - 1, None, ALU.bitwise_and)
            link(dve.tensor_scalar(hi_i[:, :], slot_i[:, :], 7, None, ALU.arith_shift_right))
            dve.tensor_copy(lo_h[:, :], lo_i[:, :])
            link(dve.tensor_copy(hi_h[:, :], hi_i[:, :]))
            dve.wait_ge(sum_step, SUM_STEPS)
            dve.reciprocal(gate[:, :], expo_sum[:, :]).then_inc(gate_ready, 1)
            for g in range(GROUPS):
                dve.tensor_tensor(tile_hots(g), iota_h[:, 0:SLOT_TILES].unsqueeze(1).to_broadcast((P, NG, SLOT_TILES)),
                                  by_tile(hi_h, g), ALU.is_equal).then_inc(hots_ready, 1)
                dve.tensor_tensor(lo_hot[:, g * NG * P:(g + 1) * NG * P].rearrange("p (n l) -> p n l", l=P),
                                  iota_h[:, :].unsqueeze(1).to_broadcast((P, NG, P)),
                                  lo_h[:, g * NG:(g + 1) * NG].unsqueeze(2).to_broadcast((P, NG, P)), ALU.is_equal)\
                    .then_inc(lo_hot_ready, 1)
            dve.wait_ge(hots_ready, GROUPS)
            dve.tensor_tensor(tile_values(GROUPS - 1, 0), tile_hots(GROUPS - 1),
                              by_tile(const[:, C_TOK:C_TOK + NP], GROUPS - 1), ALU.mult).then_inc(last_tok_ready, 1)
            link(dve.tensor_scalar(end_tile[:, :], first_slot[:, :], 1.0 / P, None, ALU.mult))
            link(dve.tensor_tensor(end_tile[:, :], end_tile[:, :], tiles_of[:, :], ALU.add))
            iota = const[:, C_IOTA:C_IOTA + P]
            link(dve.tensor_tensor(past[0:1, :].rearrange("p (s e) -> p s e", e=E),
                                   iota[0:1, 0:SLOT_TILES].unsqueeze(2).to_broadcast((1, SLOT_TILES, E)),
                                   end_tile[0:1, :].unsqueeze(1).to_broadcast((1, SLOT_TILES, E)), ALU.is_ge))
            dve.wait_ge(table_ps_ready, 1)
            dve.tensor_scalar(row_from[:, :], tab_ps[:, 0:SLOT_TILES], -1.0, 0.0, ALU.add, ALU.max).then_inc(from_ready, 1)
            link(dve.tensor_reduce(expert_f[0:1, :], past[0:1, :].rearrange("p (s e) -> p s e", e=E), AX_X, ALU.add))
            link(dve.tensor_scalar(expert_f[0:1, :], expert_f[0:1, :], float(E - 1), None, ALU.min))
            dve.tensor_copy(tiles_used[0:1, :], end_tile[0:1, E - 1:E])
            dve.tensor_scalar(expert_off[0:1, :], expert_f[0:1, :], float(WSTEP), None, ALU.mult)
            dve.tensor_scalar(load_need[0:1, :], expert_f[0:1, :], 16.0 * PIECES, 16.0 * PIECES, ALU.mult, ALU.add)
            link(dve.tensor_copy(slot_tab[:, :], tab_ps[:, 0:HV]))
            token1 = slot_tab[:, 0:SLOT_TILES]
            link(dve.tensor_scalar(empty[:, :], token1, 0.0, const[:, C_TRASH:C_TRASH + 1], ALU.is_equal, ALU.mult))
            dve.scalar_tensor_tensor(row_to[:, :], token1, -1.0, empty[:, :], ALU.add, ALU.add)\
                .then_inc(table_ready, 1)
            link(dve.scalar_tensor_tensor(slot_gate[:, :], slot_tab[:, 2 * SLOT_TILES:3 * SLOT_TILES], 1.0 / 2048.0,
                                          slot_tab[:, SLOT_TILES:2 * SLOT_TILES], ALU.mult, ALU.add))

            def gate_up(s):
                dve.wait_ge(silu_ready, s + 1)
                dve.wait_ge(up3_ready, s + 1)
                dve.tensor_tensor(act_, silu, up3_ps[:, :], ALU.mult).then_inc(act_ready, 1)

            def gate_y(s, h, wait_added=True):
                dve.wait_ge(y_ready, s + 1)
                if wait_added:
                    dve.wait_ge(y_added, 16 * (s - 1))
                dve.scalar_tensor_tensor(y_gated[h % 2], y_ps[:, 0:D], slot_gate[:, bass.ds(s, 1)], rows[h][:, D:2 * D],
                                         ALU.mult, ALU.mult).then_inc(y_gated_ready, 1)

            used = slots_used(dve)
            gate_up(0)
            gate_up(1)
            gate_y(0, 0, False)
            for s in range(2, HEAD):
                gate_up(s)
                gate_y(s - 1, (s - 1) % ROWS, s > 2)
            with dve.Fori(0, (LAST - HEAD) // UNROLL) as r:
                s0 = r * UNROLL + HEAD
                for u in range(UNROLL):
                    gate_up(s0 + u)
                    gate_y(s0 + u - 1, (HEAD + u - 1) % ROWS)
            gate_up(LAST)
            gate_y(LAST - 1, (LAST - 1) % ROWS)
            gate_y(LAST, LAST % ROWS)
            with dve.If(used > ALWAYS):
                gate_up(ALWAYS)
                for s in MORE[1:]:
                    gate_up(s)
                    gate_y(s - 1, (s - 1) % ROWS)
                gate_y(SLOT_TILES - 1, (SLOT_TILES - 1) % ROWS)


def kernel(**inputs):
    import numpy as np
    import concourse.bacc as bacc
    from concourse.bass_utils import run_bass_kernel_spmd

    def rows_by_chunk(a):
        c = a.shape[0] // P
        return np.ascontiguousarray(a.reshape(c, P, -1).transpose(1, 0, 2).reshape(P, -1))

    def experts(a):
        t = a.transpose(0, 2, 1)
        e, n, m = t.shape
        return t.reshape(e, n // P, P, m).transpose(2, 0, 1, 3).reshape(P, e, -1)

    arr = {k: np.asarray(v) for k, v in inputs.items()}
    const = np.zeros((P, C_END), np.float32)
    const[:, C_ID:C_ID + P] = np.eye(P)
    const[:, C_UP:C_UP + P] = np.triu(np.ones((P, P)), 1)
    const[:, C_IOTA:C_IOTA + P] = np.arange(P)
    const[:, C_TOK:C_TOK + 2 * TILES] = 1 + np.arange(P)[:, None] + P * np.tile(np.arange(TILES), 2)
    const[:, C_TIE:C_TIE + E] = E - np.arange(E)
    const[:, C_BEFORE:C_BEFORE + E * E] = P * np.tril(np.ones((E, E)), -1).reshape(1, -1)
    const[:, C_TRASH] = TOKENS + 1 + np.arange(P)
    feeds = {
        "x_in": np.ascontiguousarray(arr["L0_attn_x"].reshape(TOKENS, D)),
        "bT_in": rows_by_chunk(arr["L0_attn_B"].T),
        "c_in": rows_by_chunk(arr["L0_attn_C"]),
        "dT_in": rows_by_chunk(arr["L0_attn_D"].reshape(D, 1)),
        "gw_in": rows_by_chunk(arr["L0_ffn_gate_w"].T),
        "w_in": np.concatenate([experts(arr["L0_ffn_" + n]) for n in ("w1", "w3", "w2")], axis=2).reshape(P, -1),
        "cond_in": rows_by_chunk(arr["L0_c"].T),
        "wmod_in": np.concatenate([rows_by_chunk(arr["L0_wmod"][:, h * MROW:(h + 1) * MROW]) for h in range(2)], axis=1),
        "const_in": const,
    }
    nc = bacc.Bacc("TRN2", target_bir_lowering=False, num_devices=1)
    aps = [nc.dram_tensor(n, a.shape, F32, kind="ExternalInput").ap() for n, a in feeds.items()]
    out = nc.dram_tensor("out", (TOKENS + P, D), F32, kind="ExternalOutput").ap()
    build(nc, *aps, out)
    r = run_bass_kernel_spmd(nc, [feeds], core_ids=[0])
    return r.results[0]["out"][:TOKENS].reshape(BATCH, SEQ, D)
```
